# Optimizing a Trainium2 kernel written in Bass

```python
import numpy as np
import jax
import jax.numpy as jnp

def _softmax(x, axis=-1):
    return jax.nn.softmax(x, axis=axis)

def _gelu(x):
    return jax.nn.gelu(x, approximate=True)

def _silu(x):
    return jax.nn.silu(x)

def _sigmoid(x):
    return jax.nn.sigmoid(x)

def _layernorm(x, axis=-1, eps=1e-05):
    m = jnp.mean(x, axis=axis, keepdims=True)
    v = jnp.var(x, axis=axis, keepdims=True)
    return (x - m) / jnp.sqrt(v + eps)

def _scatter_add(tgt, idx, src, axis=0):
    return tgt.at[idx].add(src)

def _segment_sum(src, seg, n):
    return jax.ops.segment_sum(src, seg, n)
kernel_name = 'mk_audio_tower_d2_tok_audfeat1024_r4_6d9782'

def setup_inputs(seed: int=0):
    np.random.seed(seed)
    _w = jnp.asarray

    def _rec_inputs():
        import jax
        import jax.numpy as jnp
        _rk = jax.random.key(seed)
        x = -0.000392918 + 0.999932 * jax.random.normal(jax.random.fold_in(_rk, 1), (32, 256, 128), jnp.float32)
        return x
    x = _rec_inputs()

    def _L0_tok_setup():
        import jax, jax.numpy as jnp
        import numpy as np
        CONTEXT = 5
        DILATION = 1
        EPS = 1e-05
        key = jax.random.key(seed)
        ks = jax.random.split(key, 6)
        B, T, D, O = (32, 1024, 128, 256)
        K = D * CONTEXT
        x = jax.random.normal(ks[0], (B, T, D), dtype=jnp.float32)
        W = jax.random.normal(ks[1], (O, K), dtype=jnp.float32) * 0.02
        b = jnp.zeros((O,), dtype=jnp.float32)
        gamma = jnp.ones((O,), dtype=jnp.float32)
        beta = jnp.zeros((O,), dtype=jnp.float32)
        running_mean = jax.random.normal(ks[2], (O,), dtype=jnp.float32) * 0.1
        running_var = jax.random.uniform(ks[3], (O,), dtype=jnp.float32, minval=0.5, maxval=1.5)
        return {'x': x, 'W': W, 'b': b, 'gamma': gamma, 'beta': beta, 'running_mean': running_mean, 'running_var': running_var}
    _L0_tok_all = _L0_tok_setup()
    _L0_tok_in = {k: v for k, v in _L0_tok_all.items() if k in ('W', 'b', 'gamma', 'beta', 'running_mean', 'running_var')}
    del _L0_tok_all

    def _L0_attn_setup():
        import jax, jax.numpy as jnp
        import numpy as np
        B, L, D1, D2, N = (4, 512, 256, 256, 1024)
        key = jax.random.key(seed)
        k1, k2, k3 = jax.random.split(key, 3)
        inputs = jax.random.normal(k1, (B, L, D1), dtype=jnp.float32)
        key_param_tokens = jax.random.normal(k2, (N, D1), dtype=jnp.float32) * 0.02
        value_param_tokens = jax.random.normal(k3, (N, D2), dtype=jnp.float32) * 0.02
        return {'inputs': inputs, 'key_param_tokens': key_param_tokens, 'value_param_tokens': value_param_tokens}
    _L0_attn_all = _L0_attn_setup()
    _L0_attn_in = {k: v for k, v in _L0_attn_all.items() if k in ('key_param_tokens', 'value_param_tokens')}
    del _L0_attn_all

    def _L0_ffn_setup():
        import jax, jax.numpy as jnp
        import numpy as np
        E = 8
        TOP_K = 2
        R = 16
        ALPHA = 32.0
        SCALING = ALPHA / R
        key = jax.random.key(seed)
        k1, k2, k3, k4 = jax.random.split(key, 4)
        B, T, D_IN, D_OUT = (4, 1024, 256, 256)
        x = jax.random.normal(k1, (B, T, D_IN), dtype=jnp.float32)
        w_route = jax.random.normal(k2, (E, D_IN), dtype=jnp.float32) * 0.02
        compress = jax.random.normal(k3, (R, D_IN), dtype=jnp.float32) * 0.02
        routed = jax.random.normal(k4, (E, D_OUT, R), dtype=jnp.float32) * 0.02
        return {'x': x, 'w_route': w_route, 'compress': compress, 'routed': routed}
    _L0_ffn_all = _L0_ffn_setup()
    _L0_ffn_in = {k: v for k, v in _L0_ffn_all.items() if k in ('w_route', 'compress', 'routed')}
    del _L0_ffn_all

    def _L1_attn_setup():
        import jax, jax.numpy as jnp
        import numpy as np
        DIM = 256
        HEADS = 16
        HEAD_DIM = DIM // HEADS

        def _xavier(key, shape):
            fan_out, fan_in = shape
            limit = float(np.sqrt(6.0 / (fan_in + fan_out)))
            return jax.random.uniform(key, shape, jnp.float32, -limit, limit)
        key = jax.random.key(seed)
        kx, kv, kk, kq = jax.random.split(key, 4)
        x = jax.random.normal(kx, (4, 512, DIM), jnp.float32)
        Wv = _xavier(kv, (DIM, DIM))
        Wk = _xavier(kk, (DIM, DIM))
        Wq = _xavier(kq, (DIM, DIM))
        return {'x': x, 'Wq': Wq, 'Wk': Wk, 'Wv': Wv}
    _L1_attn_all = _L1_attn_setup()
    _L1_attn_in = {k: v for k, v in _L1_attn_all.items() if k in ('Wq', 'Wk', 'Wv')}
    del _L1_attn_all

    def _L1_ffn_setup():
        import jax, jax.numpy as jnp
        import numpy as np
        B, S, D, H, M, E, K = (4, 256, 256, 16, 2, 8, 2)
        KD = D // H
        F = 2 * D
        EPS = 1e-06

        def _ln(x, g, b):
            m = jnp.mean(x, axis=-1, keepdims=True)
            v = jnp.mean(jnp.square(x - m), axis=-1, keepdims=True)
            return (x - m) * jax.lax.rsqrt(v + EPS) * g + b
        key = jax.random.key(seed)
        ks = jax.random.split(key, 12)
        r = lambda i, shape: jax.random.normal(ks[i], shape, jnp.float32) * 0.02
        return {'x': jax.random.normal(ks[0], (B, S, D), jnp.float32), 'ln1_g': jnp.ones((D,), jnp.float32), 'ln1_b': jnp.zeros((D,), jnp.float32), 'ln2_g': jnp.ones((D,), jnp.float32), 'ln2_b': jnp.zeros((D,), jnp.float32), 'mha_wq': r(1, (M, D, H, KD)), 'mha_bq': jnp.zeros((M, H, KD), jnp.float32), 'mha_wk': r(2, (M, D, H, KD)), 'mha_bk': jnp.zeros((M, H, KD), jnp.float32), 'mha_wv': r(3, (M, D, H, KD)), 'mha_bv': jnp.zeros((M, H, KD), jnp.float32), 'mha_wo': r(4, (M, H, KD, D)), 'mha_bo': jnp.zeros((M, D), jnp.float32), 'mha_rw': r(5, (D, M)), 'mha_rb': jnp.zeros((M,), jnp.float32), 'ffn_rw': r(6, (D, E)), 'ffn_rb': jnp.zeros((E,), jnp.float32), 'fw1': r(7, (E, D, F)), 'fw2': r(8, (E, F, D))}
    _L1_ffn_all = _L1_ffn_setup()
    _L1_ffn_in = {k: v for k, v in _L1_ffn_all.items() if k in ('ln1_g', 'ln1_b', 'ln2_g', 'ln2_b', 'mha_wq', 'mha_bq', 'mha_wk', 'mha_bk', 'mha_wv', 'mha_bv', 'mha_wo', 'mha_bo', 'mha_rw', 'mha_rb', 'ffn_rw', 'ffn_rb', 'fw1', 'fw2')}
    del _L1_ffn_all
    return {'x': x, 'L0_tok_W': _L0_tok_in['W'], 'L0_tok_b': _L0_tok_in['b'], 'L0_tok_gamma': _L0_tok_in['gamma'], 'L0_tok_beta': _L0_tok_in['beta'], 'L0_tok_running_mean': _L0_tok_in['running_mean'], 'L0_tok_running_var': _L0_tok_in['running_var'], 'L0_attn_key_param_tokens': _L0_attn_in['key_param_tokens'], 'L0_attn_value_param_tokens': _L0_attn_in['value_param_tokens'], 'L0_ffn_w_route': _L0_ffn_in['w_route'], 'L0_ffn_compress': _L0_ffn_in['compress'], 'L0_ffn_routed': _L0_ffn_in['routed'], 'L1_attn_Wq': _L1_attn_in['Wq'], 'L1_attn_Wk': _L1_attn_in['Wk'], 'L1_attn_Wv': _L1_attn_in['Wv'], 'L1_ffn_ln1_g': _L1_ffn_in['ln1_g'], 'L1_ffn_ln1_b': _L1_ffn_in['ln1_b'], 'L1_ffn_ln2_g': _L1_ffn_in['ln2_g'], 'L1_ffn_ln2_b': _L1_ffn_in['ln2_b'], 'L1_ffn_mha_wq': _L1_ffn_in['mha_wq'], 'L1_ffn_mha_bq': _L1_ffn_in['mha_bq'], 'L1_ffn_mha_wk': _L1_ffn_in['mha_wk'], 'L1_ffn_mha_bk': _L1_ffn_in['mha_bk'], 'L1_ffn_mha_wv': _L1_ffn_in['mha_wv'], 'L1_ffn_mha_bv': _L1_ffn_in['mha_bv'], 'L1_ffn_mha_wo': _L1_ffn_in['mha_wo'], 'L1_ffn_mha_bo': _L1_ffn_in['mha_bo'], 'L1_ffn_mha_rw': _L1_ffn_in['mha_rw'], 'L1_ffn_mha_rb': _L1_ffn_in['mha_rb'], 'L1_ffn_ffn_rw': _L1_ffn_in['ffn_rw'], 'L1_ffn_ffn_rb': _L1_ffn_in['ffn_rb'], 'L1_ffn_fw1': _L1_ffn_in['fw1'], 'L1_ffn_fw2': _L1_ffn_in['fw2']}

def reference(x, L0_tok_W, L0_tok_b, L0_tok_gamma, L0_tok_beta, L0_tok_running_mean, L0_tok_running_var, L0_attn_key_param_tokens, L0_attn_value_param_tokens, L0_ffn_w_route, L0_ffn_compress, L0_ffn_routed, L1_attn_Wq, L1_attn_Wk, L1_attn_Wv, L1_ffn_ln1_g, L1_ffn_ln1_b, L1_ffn_ln2_g, L1_ffn_ln2_b, L1_ffn_mha_wq, L1_ffn_mha_bq, L1_ffn_mha_wk, L1_ffn_mha_bk, L1_ffn_mha_wv, L1_ffn_mha_bv, L1_ffn_mha_wo, L1_ffn_mha_bo, L1_ffn_mha_rw, L1_ffn_mha_rb, L1_ffn_ffn_rw, L1_ffn_ffn_rb, L1_ffn_fw1, L1_ffn_fw2):
    import jax
    import jax.numpy as jnp

    def _L0_tok_ref(x, W, b, gamma, beta, running_mean, running_var):
        import jax, jax.numpy as jnp
        import numpy as np
        CONTEXT = 5
        DILATION = 1
        EPS = 1e-05
        B, T, D = x.shape
        Tp = T - DILATION * (CONTEXT - 1)
        idx = jnp.arange(Tp)[:, None] + jnp.arange(CONTEXT)[None, :] * DILATION
        win = x[:, idx, :].reshape(B, Tp, CONTEXT * D)
        h = jnp.einsum('btk,ok->bto', win, W) + b
        h = jax.nn.relu(h)
        h = gamma * (h - running_mean) * jax.lax.rsqrt(running_var + EPS) + beta
        return h

    def _L0_attn_ref(inputs, key_param_tokens, value_param_tokens):
        import jax, jax.numpy as jnp
        import numpy as np
        B, L, D1, D2, N = (4, 512, 256, 256, 1024)
        attn_weight = jnp.einsum('bld,nd->bln', inputs, key_param_tokens)
        n = attn_weight.shape[-1]
        l2 = jnp.sqrt(jnp.sum(attn_weight * attn_weight, axis=-1, keepdims=True))
        normed = attn_weight / l2 * jnp.sqrt(jnp.asarray(n, attn_weight.dtype))
        attn_weight = jax.nn.gelu(normed, approximate=False)
        return jnp.einsum('bln,nd->bld', attn_weight, value_param_tokens)

    def _L0_ffn_ref(x, w_route, compress, routed):
        import jax, jax.numpy as jnp
        import numpy as np
        E = 8
        TOP_K = 2
        R = 16
        ALPHA = 32.0
        SCALING = ALPHA / R
        logits = jnp.einsum('btd,ed->bte', x, w_route)
        topk_vals, topk_idx = jax.lax.top_k(logits, TOP_K)
        topk_w = jax.nn.softmax(topk_vals, axis=-1)
        gate = jnp.sum(jax.nn.one_hot(topk_idx, E, dtype=x.dtype) * topk_w[..., None], axis=-2)
        ce = jnp.einsum('btd,rd->btr', x, compress)
        out = SCALING * jnp.einsum('btr,bte,eor->bto', ce, gate, routed)
        return out

    def _L1_attn_ref(x, Wq, Wk, Wv):
        import jax, jax.numpy as jnp
        import numpy as np
        DIM = 256
        HEADS = 16
        HEAD_DIM = DIM // HEADS

        def _xavier(key, shape):
            fan_out, fan_in = shape
            limit = float(np.sqrt(6.0 / (fan_in + fan_out)))
            return jax.random.uniform(key, shape, jnp.float32, -limit, limit)
        B, S, D = x.shape
        H, Hd = (HEADS, HEAD_DIM)
        q = (x @ Wq.T).reshape(B, S, H, Hd)
        k = (x @ Wk.T).reshape(B, S, H, Hd)
        v = (x @ Wv.T).reshape(B, S, H, Hd)
        energy = jnp.einsum('bqhd,bkhd->bhqk', q, k)
        attn = jax.nn.softmax(energy / jnp.sqrt(jnp.float32(D)), axis=-1)
        out = jnp.einsum('bhqk,bkhd->bqhd', attn, v).reshape(B, S, D)
        return out

    def _L1_ffn_ref(x, ln1_g, ln1_b, ln2_g, ln2_b, mha_wq, mha_bq, mha_wk, mha_bk, mha_wv, mha_bv, mha_wo, mha_bo, mha_rw, mha_rb, ffn_rw, ffn_rb, fw1, fw2):
        import jax, jax.numpy as jnp
        import numpy as np
        B, S, D, H, M, E, K = (4, 256, 256, 16, 2, 8, 2)
        KD = D // H
        F = 2 * D
        EPS = 1e-06

        def _ln(x, g, b):
            m = jnp.mean(x, axis=-1, keepdims=True)
            v = jnp.mean(jnp.square(x - m), axis=-1, keepdims=True)
            return (x - m) * jax.lax.rsqrt(v + EPS) * g + b
        n1 = _ln(x, ln1_g, ln1_b)
        mha_probs = jax.nn.softmax(jnp.mean(n1, axis=1) @ mha_rw + mha_rb, axis=-1)
        q = jnp.einsum('btd,mdhk->mbhtk', n1, mha_wq) + mha_bq[:, None, :, None, :]
        kk = jnp.einsum('btd,mdhk->mbhtk', n1, mha_wk) + mha_bk[:, None, :, None, :]
        v = jnp.einsum('btd,mdhk->mbhtk', n1, mha_wv) + mha_bv[:, None, :, None, :]
        scores = jnp.einsum('mbhtk,mbhsk->mbhts', q, kk) / jnp.sqrt(jnp.float32(KD))
        attn = jax.nn.softmax(scores, axis=-1)
        ctx = jnp.einsum('mbhts,mbhsk->mbthk', attn, v)
        mha_out = jnp.einsum('mbthk,mhkd->mbtd', ctx, mha_wo) + mha_bo[:, None, None, :]
        x = x + jnp.einsum('mbtd,bm->btd', mha_out, mha_probs)
        n2 = _ln(x, ln2_g, ln2_b)
        ffn_probs = jax.nn.softmax(jnp.mean(n2, axis=1) @ ffn_rw + ffn_rb, axis=-1)
        topk_p, topk_i = jax.lax.top_k(ffn_probs, K)
        topk_p = topk_p / jnp.sum(topk_p, axis=-1, keepdims=True)
        sw1 = fw1[topk_i]
        sw2 = fw2[topk_i]
        h = jax.nn.gelu(jnp.einsum('btd,bkdf->bktf', n2, sw1), approximate=False)
        eo = jnp.einsum('bktf,bkfd->bktd', h, sw2)
        return x + jnp.einsum('bktd,bk->btd', eo, topk_p)
    h = _L0_tok_ref(x, L0_tok_W, L0_tok_b, L0_tok_gamma, L0_tok_beta, L0_tok_running_mean, L0_tok_running_var)
    h = h + _L0_attn_ref(_layernorm(h, axis=-1), L0_attn_key_param_tokens, L0_attn_value_param_tokens)
    h = h + _L0_ffn_ref(_layernorm(h, axis=-1), L0_ffn_w_route, L0_ffn_compress, L0_ffn_routed)
    h = h + _L1_attn_ref(_layernorm(h, axis=-1), L1_attn_Wq, L1_attn_Wk, L1_attn_Wv)
    h = h + _L1_ffn_ref(_layernorm(h, axis=-1), L1_ffn_ln1_g, L1_ffn_ln1_b, L1_ffn_ln2_g, L1_ffn_ln2_b, L1_ffn_mha_wq, L1_ffn_mha_bq, L1_ffn_mha_wk, L1_ffn_mha_bk, L1_ffn_mha_wv, L1_ffn_mha_bv, L1_ffn_mha_wo, L1_ffn_mha_bo, L1_ffn_mha_rw, L1_ffn_mha_rb, L1_ffn_ffn_rw, L1_ffn_ffn_rb, L1_ffn_fw1, L1_ffn_fw2)
    return h

_drawn_inputs = setup_inputs


def setup_inputs(seed=0):
    import zlib

    import numpy as np

    out = dict(_drawn_inputs(seed))
    spreads = {'L0_tok_b': (0.0, 0.1),
     'L0_tok_gamma': (1.0, 0.2),
     'L0_tok_beta': (0.0, 0.1),
     'L1_ffn_ln1_g': (1.0, 0.6),
     'L1_ffn_ln1_b': (0.0, 0.8),
     'L1_ffn_ln2_g': (1.0, 0.6),
     'L1_ffn_ln2_b': (0.0, 0.614),
     'L1_ffn_mha_bq': (0.0, 2.0),
     'L1_ffn_mha_bk': (0.0, 2.0),
     'L1_ffn_mha_bv': (0.0, 0.466),
     'L1_ffn_mha_bo': (0.0, 0.1),
     'L1_ffn_mha_rb': (0.0, 2.0),
     'L1_ffn_ffn_rb': (0.0, 0.432)}
    factors = {'L1_ffn_mha_wq': 8.0, 'L1_ffn_mha_wk': 8.0, 'L1_ffn_mha_rw': 8.0}
    for name, (base, spread) in spreads.items():
        noise = np.random.default_rng([zlib.crc32(name.encode()), seed]).standard_normal(out[name].shape)
        drawn = base * np.exp(spread * noise) if base else spread * noise
        out[name] = jnp.asarray(drawn.astype(out[name].dtype))
    for name, factor in factors.items():
        out[name] = (out[name] * factor).astype(out[name].dtype)
    return out
```

```python
from contextlib import ExitStack

import concourse.bass as bass
from concourse import mybir

F32 = mybir.dt.float32
F32R = mybir.dt.float32r
I32 = mybir.dt.int32
U32 = mybir.dt.uint32
ALU = mybir.AluOpType
ACT = mybir.ActivationFunctionType
AX = mybir.AxisListType

B, T, DIN = 32, 256, 128
CONTEXT = 5
TP = T - (CONTEXT - 1)
TT = TP // 2
D = 256
DK = D // 128
NTOK = 1024
NK = NTOK // 128
E, R = 8, 16
LORA_SCALE = 32.0 / R
H, HD = 16, 16
PAIRS = H // 2
SLOTS = 4
HW = SLOTS * HD
SETS = 3
SCALE = [1.0 / 16.0, 1.0 / 4.0, 1.0 / 4.0]
VW = 32
EX = 8
F = 2 * D
FK = F // 128
EPS = 1e-5
EPS_MIX = 1e-6
PT_RING = 8

INPUTS = {
    "x": [B, T, DIN], "conv_w": [128, CONTEXT, D], "conv_rows": [5, D],
    "keys": [128, DK, NTOK], "values": [128, NK, D], "route": [128, DK, E + R], "routed": [128, D],
    "qkv_w": [128, SETS, DK, 3 * D], "qkv_bias": [2, 3 * D], "wo": [128, 2, DK, D], "bo": [2, D],
    "ln_cols": [128, 4, DK], "mix_rw": [128, DK, 2], "mix_rb": [1, 2], "ex_rw": [128, DK, EX], "ex_rb": [1, EX],
    "fw1": [128, EX, DK * F], "fw2": [128, EX, FK * D],
}

FRONT_FILLS = (["xT", "conv", "n1T"]
               + [n for tt in range(2) for n in (f"a{tt}0", f"a{tt}1", f"gT{tt}0", f"gT{tt}1", f"av{tt}")]
               + ["n2T", "rc", "cegT", "ffn"])


def set_qk(s):
    return [f"qk{s}{tt}" for tt in range(2)]


def set_v(s):
    return [f"v{s}{tt}" for tt in range(2)]


def set_stack(s):
    return [f"t{w}{s}{tt}{half}" for tt in range(2) for w in "qk" for half in range(2)]


def set_values(s):
    return [n for gg in range(2) for n in (f"o{s}{2 * gg}", f"o{s}{2 * gg + 1}", f"c{s}{gg}")]


BACK_FILLS = (["n3T"] + set_qk(0) + set_v(0) + set_stack(0) + ["mx0"] + set_values(0)
              + ["n4T", "mp"] + set_qk(1) + set_v(1) + set_stack(1) + set_qk(2) + ["mx1"] + set_stack(2)
              + set_values(1) + set_v(2) + ["cT0"] + ["mx2"] + set_values(2) + ["cT1", "wo"]
              + ["n5T", "ep"]
              + [n for tt in range(2) for n in (f"h{tt}0", f"hT{tt}0", f"h{tt}1", f"hT{tt}1", f"y{tt}")])


FRONT_AT = ((0, "scores", 0), (0, "scores", 6), (0, "scores", 8), (0, "scores", 14),
            (1, "scores", 0), (1, "scores", 6), (1, "scores", 12), (1, "attend", 4))

LOADS = 10 + 2 * EX + 11


def audio_tower(nc, inp, out):
    with ExitStack() as ctx:
        def sb(name, shape, dt=F32):
            return ctx.enter_context(nc.sbuf_tensor(name, shape, dt))

        def psum(name):
            return ctx.enter_context(nc.psum_tensor(name, [128, 512], F32))

        def sem(name):
            return ctx.enter_context(nc.semaphore(name))

        conv_w = sb("conv_w", [128, CONTEXT, D])
        conv_b = sb("conv_b", [TT, D])
        bn_a = sb("bn_a", [TT, D])
        bn_b = sb("bn_b", [TT, D])
        keys = sb("keys", [128, DK, NTOK])
        values = sb("values", [128, NK, D])
        route = sb("route", [128, DK, E + R])
        routed = sb("routed", [128, D])
        qkv_w = sb("qkv_w", [128, SETS, DK, 3 * D])
        qkv_bias = sb("qkv_bias", [TT, 2, 3 * D])
        wo = sb("wo", [128, 2, DK, D])
        bo = sb("bo", [TT, 2, D])
        ln_cols = sb("ln_cols", [128, 4, DK])
        mix_rw = sb("mix_rw", [128, DK, 2])
        mix_rb = sb("mix_rb", [128, 2])
        ex_rw = sb("ex_rw", [128, DK, EX])
        ex_rb = sb("ex_rb", [128, EX])
        fw1 = sb("fw1", [128, EX * DK * F])
        fw2 = sb("fw2", [128, EX * FK * D])
        identr = sb("identr", [128, 128], F32R)
        ident = identr[:, :].bitcast(F32)
        iota_i = sb("iota_i", [TT, E], I32)
        iota = sb("iota", [TT, E])
        neg_half = sb("neg_half", [TT, 2])

        gel_room = sb("gel_room", [128, NTOK])
        xs = gel_room[:, 0:2 * DIN].rearrange("p (t d) -> p t d", t=2)
        xT = gel_room[:, 2 * DIN:2 * DIN + T]
        nf = gel_room[0:TT, 2 * D:4 * D].rearrange("p (t d) -> p t d", t=2)
        ceg = gel_room[0:TT, 0:2 * E * R].rearrange("p (t e r) -> p t e r", t=2, e=E)
        gel = gel_room[0:TT, :]
        gelT = sb("gelT", [128, NK, TT])
        cegT = gelT[:, 0:2, :].rearrange("p k t -> p (k t)")
        hf = sb("hf", [TT, 2, D])
        nfT = sb("nfT", [128, DK, TP])
        f_stats = sb("f_stats", [TT, 2, 6])
        f_mv = sb("f_mv", [TT, 2, 2])
        f_var = sb("f_var", [TT, 2])
        f_rstd = sb("f_rstd", [TT, 2])
        ssq = sb("ssq", [TT, 2])
        ssum = sb("ssum", [TT, 1])
        smean = sb("smean", [TT, 1])
        a_scale = sb("a_scale", [TT, 2])
        rc = sb("rc", [TT, 2, E + R])
        top_v = sb("top_v", [TT, 2, 8])
        top_i = sb("top_i", [TT, 2, 8], U32)
        top_f = sb("top_f", [TT, 2, 8])
        gap = sb("gap", [TT, 2])
        gap_e = sb("gap_e", [TT, 2])
        gap_p = sb("gap_p", [TT, 2])
        w_first = sb("w_first", [TT, 2])
        w_second = sb("w_second", [TT, 2])
        gate = sb("gate", [TT, 2, E])
        gate2 = sb("gate2", [TT, 2, E])

        hb = sb("hb", [TT, 2, D])
        xm = sb("xm", [TT, 2, D])
        nb = sb("nb", [TT, 2, D])
        nbT = sb("nbT", [128, DK, TP])
        b_stats = sb("b_stats", [TT, 2, 6])
        b_mv = sb("b_mv", [TT, 2, 2])
        b_var = sb("b_var", [TT, 2])
        b_rstd = sb("b_rstd", [TT, 2])
        cx = nb[:, :, :]
        qk_room = sb("qk_room", [128, 2 * 2 * D])
        qk = qk_room[0:TT, :].rearrange("p (t w h d) -> p t w h d", t=2, w=2, h=H)
        cxT = qk_room[:, 0:2 * DK * TP].rearrange("p (m k t) -> p m k t", m=2, k=DK)
        vaug = sb("vaug", [TT, 2, H, VW])
        q_stack = sb("q_stack", [TT, H, SLOTS, HD], F32R)
        k_stack = sb("k_stack", [TT, H, SLOTS, HD], F32R)
        qT = [sb(f"qT{i}", [128, PAIRS, TP], F32R) for i in range(2)]
        kT = [sb(f"kT{i}", [128, PAIRS, TP], F32R) for i in range(2)]
        row_max = sb("row_max", [TT, 2, H])
        max_parts = sb("max_parts", [TT, 2, 2, 2, PAIRS], F32R)
        room = sb("room", [128, PT_RING * 2 * TP])
        probs = room[0:TT, :].rearrange("p (h k t) -> p h k t", h=PT_RING, k=2)
        maxT = room[0:32, (2 * PT_RING - 1) * TP:2 * PT_RING * TP]
        hid = room[0:TT, 0:F]
        hidT = room[:, F:F + 2 * FK * TT].rearrange("p (e c t) -> p e c t", e=2, c=FK)
        oT = sb("oT", [128, 2, TP])
        rec = sb("rec", [TT, 2, 8])
        msum = sb("msum", [128, DK])
        logit = sb("logit", [128, EX])
        neg_max = sb("neg_max", [128, 1])
        expo = sb("expo", [128, EX])
        esum = sb("esum", [128, 1])
        erec = sb("erec", [128, 1])
        mix_p = sb("mix_p", [128, 2])
        ex_p = sb("ex_p", [128, EX])
        ex_v = sb("ex_v", [128, 8])
        ex_i = sb("ex_i", [128, 8], U32)
        ex_o = sb("ex_o", [1, 8], I32)
        pair_sum = sb("pair_sum", [128, 1])
        pair_rec = sb("pair_rec", [128, 1])
        ex_w = sb("ex_w", [128, 2])
        y = hb[:, :, :]

        front_bank = [psum("front0"), psum("front1")]
        score_bank = [psum("score0"), psum("score1")]
        prob_bank = [psum("prob0"), psum("prob1")]
        back_bank = [psum("back0"), psum("back1")]

        loaded = sem("loaded")
        const_ready = sem("const_ready")
        front_full = [sem("front_full0"), sem("front_full1")]
        front_read = [sem("front_read0"), sem("front_read1")]
        back_full = [sem("back_full0"), sem("back_full1")]
        back_read = [sem("back_read0"), sem("back_read1")]
        x_loaded = sem("x_loaded")
        f_var_ready = sem("f_var_ready")
        f_rstd_ready = sem("f_rstd_ready")
        f_n_ready = sem("f_n_ready")
        ssq_ready = sem("ssq_ready")
        a_scale_ready = sem("a_scale_ready")
        gap_ready = sem("gap_ready")
        gap_exp_ready = sem("gap_exp_ready")
        ceg_ready = sem("ceg_ready")
        hb_copied = sem("hb_copied")
        b_var_ready = sem("b_var_ready")
        b_rstd_ready = sem("b_rstd_ready")
        b_n_ready = sem("b_n_ready")
        hi_ready = sem("hi_ready")
        lo_ready = sem("lo_ready")
        scores_full = sem("scores_full")
        maxima_done = sem("maxima_done")
        parts_ready = sem("parts_ready")
        max_placed = sem("max_placed")
        shifted_full = sem("shifted_full")
        exp_done = sem("exp_done")
        msum_ready = sem("msum_ready")
        logit_ready = sem("logit_ready")
        softexp_ready = sem("softexp_ready")
        expert_ready = sem("expert_ready")
        y_stored = sem("y_stored")
        act_chain = sem("act_chain")
        dve_chain = sem("dve_chain")
        pool_chain = sem("pool_chain")
        per_iteration = range(front_full[0].num, pool_chain.num + 1)

        FILL = {}
        for fills, banks, full, read in ((FRONT_FILLS, front_bank, front_full, front_read),
                                         (BACK_FILLS, back_bank, back_full, back_read)):
            for n, name in enumerate(fills):
                FILL[name] = (banks[n % 2], full[n % 2], read[n % 2], n // 2 + 1)

        def filled(eng, name):
            ps, full, _, n = FILL[name]
            eng.wait_ge(full, n)
            return ps

        def wait_read(eng, name):
            _, _, read, n = FILL[name]
            eng.wait_ge(read, n)

        def read_out(ins, name):
            ins.then_inc(FILL[name][2], 1)

        eye = oT[:, 0, 0:128]

        with nc.Block() as block:
            @block.sync
            def _(sp):
                for dst, name in ((conv_w, "conv_w"), (keys, "keys"), (values, "values"), (route, "route"),
                                  (routed, "routed"), (qkv_w, "qkv_w"), (wo, "wo"), (ln_cols, "ln_cols"),
                                  (mix_rw, "mix_rw"), (ex_rw, "ex_rw")):
                    shape = INPUTS[name]
                    full = (slice(None),) * len(shape)
                    sp.dma_start(dst[full], inp[name][full]).then_inc(loaded, 16)
                for e in range(EX):
                    sp.dma_start(fw1[:, e * DK * F:(e + 1) * DK * F], inp["fw1"][:, e, :]).then_inc(loaded, 16)
                    sp.dma_start(fw2[:, e * FK * D:(e + 1) * FK * D], inp["fw2"][:, e, :]).then_inc(loaded, 16)
                rows = [(conv_b[:, :], inp["conv_rows"][0:1, :]),
                        (hf[:, 0, :], inp["conv_rows"][1:2, :]), (hf[:, 1, :], inp["conv_rows"][2:3, :]),
                        (nf[:, 0, :], inp["conv_rows"][3:4, :]), (nf[:, 1, :], inp["conv_rows"][4:5, :]),
                        (mix_rb[:, :], inp["mix_rb"][0:1, :]), (ex_rb[:, :], inp["ex_rb"][0:1, :])]
                rows += [(qkv_bias[:, m, :], inp["qkv_bias"][m:m + 1, :]) for m in range(2)]
                rows += [(bo[:, m, :], inp["bo"][m:m + 1, :]) for m in range(2)]
                for dst, src in rows:
                    sp.dma_start(dst, src[0, :].partition_broadcast(dst.shape[0])).then_inc(loaded, 16)
                sp.wait_ge(loaded, 16 * LOADS)

            @block.gpsimd
            def _(pool):
                pool.memset(eye, 0.0).then_inc(const_ready, 1)
                pool.wait_ge(const_ready, 1)
                pool.affine_select(out=eye, in_=eye, compare_op=ALU.not_equal, fill=1.0, base=0,
                                   pattern=[[-1, 128]], channel_multiplier=1).then_inc(const_ready, 1)
                pool.iota(iota_i[:, :], pattern=[[1, E]], base=0, channel_multiplier=0).then_inc(const_ready, 1)
                pool.memset(neg_half[:, :], -0.5).then_inc(const_ready, 1)
                pool.memset(bn_a[:, :], -0.5).then_inc(const_ready, 1)
                pool.wait_ge(loaded, 16 * LOADS)
                pool.tensor_scalar(nf[:, 1, :], nf[:, 1, :], EPS, None, ALU.add).then_inc(pool_chain, 1)
                pool.wait_ge(pool_chain, 1)
                pool.wait_ge(const_ready, 5)
                pool.tensor_tensor(bn_a[:, :], nf[:, 1, :], bn_a[:, :], ALU.pow).then_inc(pool_chain, 1)
                pool.wait_ge(pool_chain, 2)
                pool.tensor_tensor(bn_a[:, :], bn_a[:, :], hf[:, 0, :], ALU.mult).then_inc(pool_chain, 1)
                pool.wait_ge(pool_chain, 3)
                pool.tensor_tensor(nf[:, 0, :], nf[:, 0, :], bn_a[:, :], ALU.mult).then_inc(pool_chain, 1)
                pool.wait_ge(pool_chain, 4)
                pool.tensor_tensor(bn_b[:, :], hf[:, 1, :], nf[:, 0, :], ALU.subtract).then_inc(pool_chain, 1)

            @block.vector
            def _(dve):
                dve.wait_ge(const_ready, 3)
                dve.tensor_copy(identr[:, :], eye)
                dve.tensor_copy(iota[:, :], iota_i[:, :])
                dve.memset(q_stack[:, :, 3, :].bitcast(F32), 0.0)
                dve.memset(k_stack[:, :, 3, 2:HD].bitcast(F32), 0.0)
                dve.memset(k_stack[:, :, 3, 0:2].bitcast(F32), -1.0)
                dve.memset(vaug[:, :, :, HD:VW], 1.0)

        nc.all_engine_barrier(sems_to_clear=per_iteration)

        def iteration(front, back):
            F_ON, B_ON = front is not None, back is not None

            def steps_at(where):
                return [n for n, at in enumerate(FRONT_AT) if at == where] if F_ON else []

            with nc.Block(no_gpsimd_drain=True) as block:
                @block.sync
                def _(sp):
                    if F_ON:
                        sp.dma_start(xs, inp["x"][front, :, :].rearrange("(t p) d -> p t d", p=128))\
                          .then_inc(x_loaded, 16)
                    if B_ON:
                        for st in range(SETS):
                            wait_read(sp, f"mx{st}")
                            for j in range(2):
                                for part in range(2):
                                    r = 8 * (2 * j + part)
                                    row = HW * j + 3 * HD + part
                                    sp.dma_start(qT[st % 2][row:row + 1, :, :].bitcast(F32),
                                                 maxT[r:r + 8, :])\
                                      .then_inc(max_placed, 16)
                        wait_read(sp, "y0")
                        wait_read(sp, "y1")
                        sp.dma_start(out[back, :, :].rearrange("(t p) d -> p t d", p=TT), y)\
                          .then_inc(y_stored, 16)
                        sp.wait_ge(y_stored, 16)
                    if F_ON:
                        sp.wait_ge(x_loaded, 16)

                @block.tensor
                def _(pe):
                    def take(name):
                        ps, _, read, n = FILL[name]
                        if n > 1:
                            pe.wait_ge(read, n - 1)
                        return ps

                    def done(name, ins):
                        ins.then_inc(FILL[name][1], 1)

                    def turn(name, src):
                        ps = take(name)
                        for tt in range(2):
                            for k in range(DK):
                                c = k * TP + tt * TT
                                last = pe.transpose(ps[:, c:c + TT], src[:, tt, k * 128:(k + 1) * 128],
                                                    ident[0:TT, 0:TT])
                        done(name, last)

                    def front_step(n):
                        if n == 0:
                            pe.wait_ge(x_loaded, 16)
                            ps = take("xT")
                            for t in range(2):
                                last = pe.transpose(ps[:, t * 128:(t + 1) * 128], xs[:, t, :], ident)
                            done("xT", last)
                            ps = take("conv")
                            wait_read(pe, "xT")
                            for tt in range(2):
                                for c in range(CONTEXT):
                                    last = pe.matmul(ps[0:TT, tt * D:(tt + 1) * D], xT[:, tt * TT + c:tt * TT + c + TT],
                                                     conv_w[:, c, :], start=c == 0, stop=c == CONTEXT - 1)
                            done("conv", last)
                        if n == 1:
                            pe.wait_ge(f_n_ready, 1)
                            turn("n1T", nf)
                        if n in (2, 4):
                            tt = (n - 2) // 2
                            wait_read(pe, "n1T")
                            for half in range(2):
                                ps = take(f"a{tt}{half}")
                                for k in range(DK):
                                    last = pe.matmul(ps[0:TT, :], nfT[:, k, tt * TT:(tt + 1) * TT],
                                                     keys[:, k, half * 512:(half + 1) * 512],
                                                     start=k == 0, stop=k == DK - 1)
                                done(f"a{tt}{half}", last)
                        if n in (3, 5):
                            tt = (n - 3) // 2
                            for half in range(2):
                                wait_read(pe, f"a{tt}{half}")
                                ps = take(f"gT{tt}{half}")
                                for c in range(4):
                                    blk = 4 * half + c
                                    last = pe.transpose(ps[:, c * TT:(c + 1) * TT], gel[:, blk * 128:(blk + 1) * 128],
                                                        ident[0:TT, 0:TT])
                                done(f"gT{tt}{half}", last)
                            ps = take(f"av{tt}")
                            wait_read(pe, f"gT{tt}0")
                            wait_read(pe, f"gT{tt}1")
                            for blk in range(NK):
                                last = pe.matmul(ps[0:TT, 0:D], gelT[:, blk, :], values[:, blk, :],
                                                 start=blk == 0, stop=blk == NK - 1)
                            done(f"av{tt}", last)
                        if n == 6:
                            pe.wait_ge(f_n_ready, 2)
                            turn("n2T", nf)
                            ps = take("rc")
                            wait_read(pe, "n2T")
                            for tt in range(2):
                                for k in range(DK):
                                    last = pe.matmul(ps[0:TT, tt * 32:tt * 32 + E + R],
                                                     nfT[:, k, tt * TT:(tt + 1) * TT], route[:, k, :],
                                                     start=k == 0, stop=k == DK - 1)
                            done("rc", last)
                        if n == 7:
                            pe.wait_ge(ceg_ready, 1)
                            ps = take("cegT")
                            for tt in range(2):
                                last = pe.transpose(ps[:, tt * TT:(tt + 1) * TT],
                                                    ceg[:, tt, :, :].rearrange("p e r -> p (e r)"), ident[0:TT, 0:TT])
                            done("cegT", last)
                            ps = take("ffn")
                            wait_read(pe, "cegT")
                            for tt in range(2):
                                last = pe.matmul(ps[0:TT, tt * D:(tt + 1) * D], cegT[:, tt * TT:(tt + 1) * TT],
                                                 routed[:, :], start=True, stop=True)
                            done("ffn", last)

                    def project(st, what):
                        lo, hi = {"qk": (0, 2 * D), "v": (2 * D, 3 * D)}[what]
                        for tt in range(2):
                            ps = take(f"{what}{st}{tt}")
                            for k in range(DK):
                                last = pe.matmul(ps[0:TT, 0:hi - lo], nbT[:, k, tt * TT:(tt + 1) * TT],
                                                 qkv_w[:, st, k, lo:hi], start=k == 0, stop=k == DK - 1)
                            done(f"{what}{st}{tt}", last)

                    def stack_columns(st):
                        for tt in range(2):
                            pe.wait_ge(hi_ready, 2 * (2 * st + tt + 1))
                            pe.wait_ge(lo_ready, 2 * (2 * st + tt + 1))
                            for w, src in (("q", q_stack), ("k", k_stack)):
                                for half in range(2):
                                    name = f"t{w}{st}{tt}{half}"
                                    ps = take(name)
                                    for c in range(4):
                                        p = 4 * half + c
                                        last = pe.transpose(ps[:, c * TT:(c + 1) * TT].bitcast(F32R),
                                                            src[:, 2 * p:2 * p + 2, :, :].rearrange("q h s d -> q (h s d)"),
                                                            identr[0:TT, 0:TT])
                                    done(name, last)

                    def scores(st, h):
                        n = H * st + h
                        if h == 0:
                            for tt in range(2):
                                for w in "qk":
                                    for half in range(2):
                                        wait_read(pe, f"t{w}{st}{tt}{half}")
                        if n >= 2:
                            pe.wait_ge(maxima_done, n - 1)
                        p, r = h // 2, HW * (h % 2)
                        for tt in range(2):
                            last = pe.matmul(score_bank[n % 2][0:TT, tt * TP:(tt + 1) * TP],
                                             qT[st % 2][r:r + HW, p, tt * TT:(tt + 1) * TT],
                                             kT[st % 2][r:r + HW, p, :], start=True, stop=True)
                        last.then_inc(scores_full, 1)

                    def max_columns(st):
                        pe.wait_ge(parts_ready, st + 1)
                        ps = take(f"mx{st}")
                        for tt in range(2):
                            last = pe.transpose(ps[0:32, tt * TT:(tt + 1) * TT].bitcast(F32R),
                                                max_parts[:, tt, :, :, :].rearrange("q j s p -> q (j s p)"),
                                                identr[0:TT, 0:TT])
                        done(f"mx{st}", last)

                    def shifted(st, h):
                        n = H * st + h
                        if h == 0:
                            pe.wait_ge(max_placed, 64 * (st + 1))
                        if n >= 2:
                            pe.wait_ge(exp_done, n - 1)
                        p, r = h // 2, HW * (h % 2)
                        for tt in range(2):
                            last = pe.matmul(prob_bank[n % 2][0:TT, tt * TP:(tt + 1) * TP],
                                             kT[st % 2][r:r + HW, p, tt * TT:(tt + 1) * TT],
                                             qT[st % 2][r:r + HW, p, :], start=True, stop=True)
                        last.then_inc(shifted_full, 1)

                    def weighted_values(st, g):
                        pe.wait_ge(exp_done, H * st + 4 * g + 4)
                        if g == 0:
                            wait_read(pe, f"v{st}0")
                            wait_read(pe, f"v{st}1")
                        ps = take(f"o{st}{g}")
                        for tt in range(2):
                            for c in range(4):
                                h = 4 * g + c
                                last = pe.matmul(ps[32 * c:32 * c + 32, 0:TP], vaug[:, tt, h, :],
                                                 probs[:, h % PT_RING, tt, :], start=tt == 0, stop=tt == 1,
                                                 skip_group_check=True)
                        done(f"o{st}{g}", last)

                    def context_rows(st, gg):
                        wait_read(pe, f"o{st}{2 * gg}")
                        wait_read(pe, f"o{st}{2 * gg + 1}")
                        ps = take(f"c{st}{gg}")
                        for g in range(2):
                            for tt in range(2):
                                c = (2 * tt + g) * 128
                                last = pe.transpose(ps[0:TT, c:c + 128], oT[:, g, tt * TT:(tt + 1) * TT], ident)
                        done(f"c{st}{gg}", last)

                    def score_all(st):
                        for h in range(H):
                            scores(st, h)
                            for n in steps_at((st, "scores", h)):
                                front_step(n)
                        max_columns(st)

                    def attend(st, beside=None):
                        for h in range(H):
                            shifted(st, h)
                            if beside is not None:
                                scores(beside, h)
                            for n in steps_at((st, "attend", h)):
                                front_step(n)
                            if h % 4 == 3 and h > 3:
                                weighted_values(st, h // 4 - 1)
                            if h == 11:
                                context_rows(st, 0)
                        weighted_values(st, 3)
                        context_rows(st, 1)

                    def logits(name, w, n, count):
                        pe.wait_ge(msum_ready, count)
                        ps = take(name)
                        for k in range(DK):
                            last = pe.matmul(ps[:, 0:n], msum[:, k:k + 1].broadcast_to([128, 128]), w[:, k, :],
                                             start=k == 0, stop=k == DK - 1)
                        done(name, last)

                    if not B_ON:
                        for n in range(8):
                            front_step(n)
                        return
                    pe.wait_ge(b_n_ready, 1)
                    turn("n3T", nb)
                    wait_read(pe, "n3T")
                    project(0, "qk")
                    project(0, "v")
                    stack_columns(0)
                    score_all(0)
                    attend(0)

                    pe.wait_ge(b_n_ready, 3)
                    turn("n4T", nb)
                    wait_read(pe, "n4T")
                    logits("mp", mix_rw, 2, 1)
                    project(1, "qk")
                    project(1, "v")
                    stack_columns(1)
                    project(2, "qk")
                    score_all(1)
                    stack_columns(2)
                    attend(1, beside=2)
                    project(2, "v")
                    wait_read(pe, "c10")
                    wait_read(pe, "c11")
                    turn("cT0", cx)
                    max_columns(2)
                    attend(2)
                    wait_read(pe, "c20")
                    wait_read(pe, "c21")
                    turn("cT1", cx)
                    ps = take("wo")
                    wait_read(pe, "cT0")
                    wait_read(pe, "cT1")
                    for tt in range(2):
                        for m in range(2):
                            for k in range(DK):
                                last = pe.matmul(ps[0:TT, tt * D:(tt + 1) * D], cxT[:, m, k, tt * TT:(tt + 1) * TT],
                                                 wo[:, m, k, :], start=m + k == 0, stop=m + k == DK)
                    done("wo", last)

                    pe.wait_ge(b_n_ready, 4)
                    turn("n5T", nb)
                    wait_read(pe, "n5T")
                    logits("ep", ex_rw, EX, 2)
                    pe.wait_ge(expert_ready, 1)
                    ex = [pe.value_load(ex_o[0:1, k:k + 1], min_val=0, max_val=EX - 1) for k in range(2)]
                    for tt in range(2):
                        for k in range(2):
                            ps = take(f"h{tt}{k}")
                            for d in range(DK):
                                last = pe.matmul(ps[0:TT, :], nbT[:, d, tt * TT:(tt + 1) * TT],
                                                 fw1[:, bass.ds(ex[k] * (DK * F) + d * F, F)],
                                                 start=d == 0, stop=d == DK - 1)
                            done(f"h{tt}{k}", last)
                            wait_read(pe, f"h{tt}{k}")
                            ps = take(f"hT{tt}{k}")
                            for c in range(FK):
                                last = pe.transpose(ps[:, c * TT:(c + 1) * TT], hid[:, c * 128:(c + 1) * 128],
                                                    ident[0:TT, 0:TT])
                            done(f"hT{tt}{k}", last)
                        ps = take(f"y{tt}")
                        wait_read(pe, f"hT{tt}0")
                        wait_read(pe, f"hT{tt}1")
                        for k in range(2):
                            for c in range(FK):
                                last = pe.matmul(ps[0:TT, 0:D], hidT[:, k, c, :],
                                                 fw2[:, bass.ds(ex[k] * (FK * D) + c * D, D)],
                                                 start=k + c == 0, stop=k + c == FK)
                        done(f"y{tt}", last)

                @block.scalar
                def _(act):
                    def columns(ps):
                        return ps[:, 0:DK * TP].rearrange("p (k t) -> p k t", k=DK)

                    def front_step(n):
                        if n == 0:
                            ps = filled(act, "xT")
                            read_out(act.copy(xT, ps[:, 0:T]), "xT")
                        if n == 1:
                            ps = filled(act, "n1T")
                            read_out(act.copy(nfT[:, :, :], columns(ps)), "n1T")
                        if n in (2, 4):
                            tt = (n - 2) // 2
                            if tt:
                                filled(act, "gT00")
                                filled(act, "gT01")
                            for half in range(2):
                                ps = filled(act, f"a{tt}{half}")
                                act.activation(gel[:, half * 512:(half + 1) * 512], ps[0:TT, :], ACT.Square,
                                               accum_out=ssq[:, half:half + 1]).then_inc(ssq_ready, 1)
                            act.wait_ge(ssq_ready, 2 * tt + 2)
                            act.wait_ge(a_scale_ready, tt + 1)
                            for half in range(2):
                                ps = FILL[f"a{tt}{half}"][0]
                                read_out(act.activation(gel[:, half * 512:(half + 1) * 512], ps[0:TT, :], ACT.Gelu,
                                                        scale=a_scale[:, tt:tt + 1]), f"a{tt}{half}")
                        if n == 6:
                            ps = filled(act, "n2T")
                            read_out(act.copy(nfT[:, :, :], columns(ps)), "n2T")
                            act.wait_ge(gap_ready, 1)
                            act.activation(gap_e[:, :], gap[:, :], ACT.Exp).then_inc(gap_exp_ready, 1)
                        if n == 7:
                            ps = filled(act, "cegT")
                            read_out(act.copy(cegT[:, :], ps[:, 0:TP]), "cegT")

                    def hi_parts(st, tt):
                        wait_read(act, f"qk{st}{tt}")
                        if (st, tt) != (0, 0):
                            before = 2 * st + tt - 1
                            filled(act, f"tq{before // 2}{before % 2}1")
                            filled(act, f"tk{before // 2}{before % 2}1")
                        act.copy(q_stack[:, :, 0:2, :],
                                 qk[:, tt, 0, :, :].unsqueeze(2).broadcast_to([TT, H, 2, HD])).then_inc(hi_ready, 1)
                        act.copy(k_stack[:, :, 0:3:2, :],
                                 qk[:, tt, 1, :, :].unsqueeze(2).broadcast_to([TT, H, 2, HD])).then_inc(hi_ready, 1)

                    def query_columns(st, tt):
                        for half in range(2):
                            name = f"tq{st}{tt}{half}"
                            ps = filled(act, name)
                            read_out(act.copy(qT[st % 2][:, 4 * half:4 * half + 4, tt * TT:(tt + 1) * TT],
                                              ps[:, 0:4 * TT].rearrange("p (c t) -> p c t", c=4)), name)

                    def max_rows(st):
                        ps = filled(act, f"mx{st}")
                        if st:
                            act.wait_ge(max_placed, 64 * st)
                        read_out(act.copy(maxT, ps[0:32, 0:TP]), f"mx{st}")

                    def exp_head(st, h):
                        n = H * st + h
                        act.wait_ge(shifted_full, n + 1)
                        if n % 4 == 0 and n >= PT_RING:
                            g = n // 4 - 2
                            filled(act, f"o{g // 4}{g % 4}")
                        act.activation(probs[:, h % PT_RING, :, :],
                                       prob_bank[n % 2][0:TT, 0:2 * TP].rearrange("p (k t) -> p k t", k=2),
                                       ACT.Exp, scale=SCALE[st]).then_inc(exp_done, 1)

                    def values_out(st, g):
                        ps = filled(act, f"o{st}{g}")
                        if g >= 2:
                            filled(act, f"c{st}0")
                        elif st:
                            filled(act, f"c{st - 1}1")
                        read_out(act.copy(oT[:, g % 2, :], ps[:, 0:TP]), f"o{st}{g}")

                    def attend(st):
                        for h in range(H):
                            exp_head(st, h)
                            for n in steps_at((st, "attend", h)):
                                front_step(n)
                            if st == 1 and h % 4 == 3 and h > 3:
                                values_out(st, h // 4 - 1)
                        if st == 1:
                            values_out(st, 3)

                    def front_beside(st):
                        for h in range(H):
                            for n in steps_at((st, "scores", h)):
                                front_step(n)

                    def gained_columns(name, i):
                        ps = filled(act, name)
                        for k in range(DK):
                            last = act.activation(nbT[:, k, :], ps[:, k * TP:(k + 1) * TP], ACT.Identity,
                                                  scale=ln_cols[:, i, k:k + 1], bias=ln_cols[:, i + 1, k:k + 1])
                        read_out(last, name)

                    def soft_exp(n, count):
                        act.wait_ge(logit_ready, count)
                        act.activation(expo[:, 0:n], logit[:, 0:n], ACT.Exp, bias=neg_max[:, :],
                                       accum_out=esum[:, :]).then_inc(softexp_ready, 1)

                    if not B_ON:
                        for n in range(8):
                            front_step(n)
                        return
                    act.copy(hb[:, :, :], hf[:, :, :]).then_inc(hb_copied, 1)
                    ps = filled(act, "n3T")
                    read_out(act.copy(nbT[:, :, :], columns(ps)), "n3T")
                    for tt in range(2):
                        ps = filled(act, f"qk0{tt}")
                        read_out(act.copy(qk[:, tt, :, :, :].rearrange("p w h d -> p (w h d)"), ps[0:TT, :]), f"qk0{tt}")
                        if tt == 0:
                            hi_parts(0, 0)
                    query_columns(0, 0)
                    hi_parts(0, 1)
                    query_columns(0, 1)
                    front_beside(0)
                    max_rows(0)
                    attend(0)

                    gained_columns("n4T", 0)
                    soft_exp(2, 1)
                    hi_parts(1, 0)
                    query_columns(1, 0)
                    hi_parts(1, 1)
                    query_columns(1, 1)
                    hi_parts(2, 0)
                    front_beside(1)
                    max_rows(1)
                    query_columns(2, 0)
                    hi_parts(2, 1)
                    query_columns(2, 1)
                    attend(1)
                    ps = filled(act, "cT0")
                    read_out(act.copy(cxT[:, 0, :, :], columns(ps)), "cT0")
                    max_rows(2)
                    attend(2)
                    ps = filled(act, "cT1")
                    read_out(act.copy(cxT[:, 1, :, :], columns(ps)), "cT1")

                    gained_columns("n5T", 2)
                    soft_exp(EX, 2)
                    before = None
                    for tt in range(2):
                        for k in range(2):
                            ps = filled(act, f"h{tt}{k}")
                            if before:
                                filled(act, before)
                            read_out(act.activation(hid[:, :], ps[0:TT, :], ACT.Gelu), f"h{tt}{k}")
                            before = f"hT{tt}{k}"

                @block.vector
                def _(dve):
                    chain = [0]

                    def link(ins):
                        chain[0] += 1
                        ins.then_inc(dve_chain, 1)
                        dve.wait_ge(dve_chain, chain[0])

                    def layer_norm(h, n, stats, mv, var_ready, rstd, rstd_ready, n_ready, count):
                        for tt in range(2):
                            last = dve.bn_stats(stats[:, tt, :], h[:, tt, :])
                        link(last)
                        for tt in range(2):
                            last = dve.bn_aggr(mv[:, tt, :], stats[:, tt, :])
                        last.then_inc(var_ready, 1)
                        dve.wait_ge(var_ready, count)
                        dve.wait_ge(rstd_ready, count)
                        for tt in range(2):
                            last = dve.tensor_scalar(n[:, tt, :], h[:, tt, :], mv[:, tt, 0:1], rstd[:, tt:tt + 1],
                                                     ALU.subtract, ALU.mult)
                        last.then_inc(n_ready, 1)

                    def front_norm(count):
                        layer_norm(hf, nf, f_stats, f_mv, f_var_ready, f_rstd, f_rstd_ready, f_n_ready, count)

                    def back_norm(count, h=hb, n=nb):
                        layer_norm(h, n, b_stats, b_mv, b_var_ready, b_rstd, b_rstd_ready, b_n_ready, count)

                    def both(row):
                        return row.unsqueeze(1).broadcast_to([TT, 2, D])

                    def front_step(n):
                        if n == 0:
                            ps = filled(dve, "conv")
                            if B_ON:
                                dve.wait_ge(hb_copied, 1)
                            read_out(dve.tensor_tensor(hf[:, :, :], ps[0:TT, :].rearrange("p (t d) -> p t d", t=2),
                                                       both(conv_b[:, :]), ALU.add), "conv")
                            wait_read(dve, "conv")
                            link(dve.scalar_tensor_tensor(hf[:, :, :], hf[:, :, :], 0.0, both(bn_a[:, :]),
                                                          ALU.max, ALU.mult))
                            link(dve.tensor_tensor(hf[:, :, :], hf[:, :, :], both(bn_b[:, :]), ALU.add))
                            front_norm(1)
                        if n in (3, 5):
                            tt = (n - 3) // 2
                            if tt:
                                filled(dve, "av0")
                            for half in range(2):
                                ps = filled(dve, f"gT{tt}{half}")
                                read_out(dve.tensor_copy(gelT[:, 4 * half:4 * half + 4, :],
                                                         ps[:, 0:4 * TT].rearrange("p (c t) -> p c t", c=4)),
                                         f"gT{tt}{half}")
                            ps = filled(dve, f"av{tt}")
                            read_out(dve.tensor_tensor(hf[:, tt, :], hf[:, tt, :], ps[0:TT, 0:D], ALU.add), f"av{tt}")
                            if tt:
                                wait_read(dve, "av0")
                                wait_read(dve, "av1")
                                front_norm(2)
                        if n == 6:
                            ps = filled(dve, "rc")
                            read_out(dve.tensor_copy(rc[:, :, :], ps[0:TT, 0:64].rearrange("p (t c) -> p t c", t=2)
                                                     [:, :, 0:E + R]), "rc")
                            wait_read(dve, "rc")
                            for tt in range(2):
                                last = dve.max(top_v[:, tt, :], rc[:, tt, 0:E])
                            link(last)
                            dve.tensor_tensor(gap[:, :], top_v[:, :, 1], top_v[:, :, 0], ALU.subtract)\
                               .then_inc(gap_ready, 1)
                            for tt in range(2):
                                last = dve.max_index(top_i[:, tt, :], top_v[:, tt, :], rc[:, tt, 0:E])
                            link(last)
                            link(dve.tensor_copy(top_f[:, :, :], top_i[:, :, :]))
                            dve.wait_ge(gap_exp_ready, 1)
                            link(dve.tensor_scalar(gap_p[:, :], gap_e[:, :], 1.0, None, ALU.add))
                            link(dve.reciprocal(w_first[:, :], gap_p[:, :]))
                            link(dve.tensor_tensor(w_second[:, :], gap_e[:, :], w_first[:, :], ALU.mult))
                            for tt in range(2):
                                dve.tensor_scalar(gate[:, tt, :], iota[:, :], top_f[:, tt, 0:1], w_first[:, tt:tt + 1],
                                                  ALU.is_equal, ALU.mult)
                                last = dve.tensor_scalar(gate2[:, tt, :], iota[:, :], top_f[:, tt, 1:2],
                                                         w_second[:, tt:tt + 1], ALU.is_equal, ALU.mult)
                            link(last)
                            link(dve.tensor_tensor(gate[:, :, :], gate[:, :, :], gate2[:, :, :], ALU.add))
                            dve.tensor_tensor(ceg[:, :, :, :], gate[:, :, :].unsqueeze(3).broadcast_to([TT, 2, E, R]),
                                              rc[:, :, E:E + R].unsqueeze(2).broadcast_to([TT, 2, E, R]),
                                              ALU.mult).then_inc(ceg_ready, 1)
                        if n == 7:
                            ps = filled(dve, "ffn")
                            read_out(dve.scalar_tensor_tensor(hf[:, :, :], ps[0:TT, :].rearrange("p (t d) -> p t d", t=2),
                                                              LORA_SCALE, hf[:, :, :], ALU.mult, ALU.add), "ffn")

                    def key_columns(st, tt):
                        for half in range(2):
                            name = f"tk{st}{tt}{half}"
                            ps = filled(dve, name)
                            read_out(dve.tensor_copy(kT[st % 2][:, 4 * half:4 * half + 4, tt * TT:(tt + 1) * TT],
                                                     ps[:, 0:4 * TT].rearrange("p (c t) -> p c t", c=4)), name)

                    def values_in(st, tt):
                        name = f"v{st}{tt}"
                        ps = filled(dve, name)
                        if st:
                            filled(dve, f"o{st - 1}3")
                        rows = ps[0:TT, 0:D].rearrange("p (h d) -> p h d", h=H)
                        dst = vaug[:, tt, :, 0:HD]
                        if st == 0:
                            read_out(dve.tensor_copy(dst, rows), name)
                        else:
                            bias = qkv_bias[:, st - 1, 2 * D:3 * D].rearrange("p (h d) -> p h d", h=H)
                            read_out(dve.tensor_tensor(dst, rows, bias, ALU.add), name)

                    def queries_keys_in(st, tt):
                        name = f"qk{st}{tt}"
                        ps = filled(dve, name)
                        dve.wait_ge(lo_ready, 2 * (2 * (st - 1) + tt + 1))
                        read_out(dve.tensor_tensor(qk[:, tt, :, :, :].rearrange("p w h d -> p (w h d)"), ps[0:TT, :],
                                                   qkv_bias[:, st - 1, 0:2 * D], ALU.add), name)

                    def maximum(st, h):
                        n = H * st + h
                        dve.wait_ge(scores_full, n + 1)
                        dve.tensor_reduce(row_max[:, :, h], score_bank[n % 2][0:TT, 0:2 * TP]
                                          .rearrange("p (t k) -> p t k", t=2), AX.X, ALU.max).then_inc(maxima_done, 1)

                    def split_maxima(st):
                        dve.wait_ge(maxima_done, H * (st + 1))
                        if st:
                            filled(dve, f"mx{st - 1}")
                        src = row_max[:, :, :].rearrange("q t (p j) -> q t j p", j=2)
                        link(dve.tensor_copy(max_parts[:, :, :, 0, :], src))
                        dve.tensor_tensor(max_parts[:, :, :, 1, :], src, max_parts[:, :, :, 0, :].bitcast(F32),
                                          ALU.subtract).then_inc(parts_ready, 1)

                    def values_out(st, g):
                        ps = filled(dve, f"o{st}{g}")
                        if g >= 2:
                            filled(dve, f"c{st}0")
                        elif st:
                            filled(dve, f"c{st - 1}1")
                        read_out(dve.tensor_copy(oT[:, g % 2, :], ps[:, 0:TP]), f"o{st}{g}")

                    def context(st, gg):
                        name = f"c{st}{gg}"
                        ps = filled(dve, name)
                        rows = ps[0:TT, :].rearrange("p (t h w) -> p t h w", t=2, w=VW)
                        link(dve.reciprocal(rec[:, :, :], rows[:, :, :, HD]))
                        if st:
                            link(dve.tensor_scalar(rec[:, :, :], rec[:, :, :], mix_p[0:TT, st - 1:st], None, ALU.mult))
                        if st == 2 and gg == 0:
                            filled(dve, "cT0")
                        dst = cx[:, :, :].rearrange("p t (h d) -> p t h d", d=HD)[:, :, 8 * gg:8 * gg + 8, :]
                        read_out(dve.tensor_tensor(dst, rows[:, :, :, 0:HD],
                                                   rec[:, :, :].unsqueeze(3).broadcast_to([TT, 2, 8, HD]),
                                                   ALU.mult), name)

                    def score_all(st):
                        for h in range(H):
                            maximum(st, h)
                            for n in steps_at((st, "scores", h)):
                                front_step(n)
                        split_maxima(st)

                    def attend(st, beside=None):
                        for h in range(H):
                            if beside is not None:
                                maximum(beside, h)
                            for n in steps_at((st, "attend", h)):
                                front_step(n)
                            if st != 1 and h % 4 == 3 and h > 3:
                                values_out(st, h // 4 - 1)
                            if h == 11:
                                context(st, 0)
                        if beside is not None:
                            split_maxima(beside)
                        if st != 1:
                            values_out(st, 3)
                        context(st, 1)
                        wait_read(dve, f"c{st}0")
                        wait_read(dve, f"c{st}1")

                    def mean_columns(name):
                        wait_read(dve, name)
                        dve.tensor_reduce(msum[:, :], nbT[:, :, :], AX.X, ALU.add).then_inc(msum_ready, 1)

                    def softmax(name, n, bias, p, count):
                        ps = filled(dve, name)
                        read_out(dve.scalar_tensor_tensor(logit[:, 0:n], ps[:, 0:n], 1.0 / TP, bias[:, 0:n],
                                                          ALU.mult, ALU.add), name)
                        wait_read(dve, name)
                        dve.tensor_reduce(neg_max[:, :], logit[:, 0:n], AX.X, ALU.max, negate=True)\
                           .then_inc(logit_ready, 1)
                        dve.wait_ge(softexp_ready, count)
                        link(dve.reciprocal(erec[:, :], esum[:, :]))
                        link(dve.tensor_scalar(p[:, 0:n], expo[:, 0:n], erec[:, 0:1], None, ALU.mult))

                    if not B_ON:
                        for n in range(8):
                            front_step(n)
                        return
                    dve.wait_ge(hb_copied, 1)
                    back_norm(1)
                    values_in(0, 0)
                    values_in(0, 1)
                    key_columns(0, 0)
                    key_columns(0, 1)
                    score_all(0)
                    attend(0)
                    link(dve.tensor_tensor(hb[:, :, :], hb[:, :, :], cx[:, :, :], ALU.add))
                    back_norm(2, hb, xm)
                    dve.wait_ge(b_n_ready, 2)
                    back_norm(3, xm, nb)
                    mean_columns("n4T")
                    softmax("mp", 2, mix_rb, mix_p, 1)
                    for m in range(2):
                        link(dve.scalar_tensor_tensor(xm[:, :, :], both(bo[:, m, :]), mix_p[0:TT, m:m + 1],
                                                      xm[:, :, :], ALU.mult, ALU.add))
                    queries_keys_in(1, 0)
                    queries_keys_in(1, 1)
                    values_in(1, 0)
                    values_in(1, 1)
                    key_columns(1, 0)
                    key_columns(1, 1)
                    queries_keys_in(2, 0)
                    queries_keys_in(2, 1)
                    score_all(1)
                    key_columns(2, 0)
                    key_columns(2, 1)
                    attend(1, beside=2)
                    values_in(2, 0)
                    values_in(2, 1)
                    attend(2)
                    ps = filled(dve, "wo")
                    read_out(dve.tensor_tensor(xm[:, :, :], xm[:, :, :], ps[0:TT, :].rearrange("p (t d) -> p t d", t=2),
                                               ALU.add), "wo")
                    wait_read(dve, "wo")
                    back_norm(4, xm, nb)
                    link(dve.tensor_tensor(hb[:, :, :], hb[:, :, :], xm[:, :, :], ALU.add))
                    mean_columns("n5T")
                    softmax("ep", EX, ex_rb, ex_p, 2)
                    link(dve.max(ex_v[:, :], ex_p[:, :]))
                    link(dve.max_index(ex_i[:, :], ex_v[:, :], ex_p[:, :]))
                    dve.tensor_copy(ex_o[:, :], ex_i[0:1, :]).then_inc(expert_ready, 1)
                    link(dve.tensor_tensor(pair_sum[:, :], ex_v[:, 0:1], ex_v[:, 1:2], ALU.add))
                    link(dve.reciprocal(pair_rec[:, :], pair_sum[:, :]))
                    link(dve.tensor_scalar(ex_w[:, :], ex_v[:, 0:2], pair_rec[:, 0:1], None, ALU.mult))
                    for tt in range(2):
                        for k in range(2):
                            name = f"hT{tt}{k}"
                            ps = filled(dve, name)
                            if tt and not k:
                                filled(dve, "y0")
                            read_out(dve.tensor_scalar(hidT[:, k, :, :], ps[:, 0:FK * TT].rearrange("p (c t) -> p c t", c=FK),
                                                       ex_w[:, k:k + 1], None, ALU.mult), name)
                        ps = filled(dve, f"y{tt}")
                        read_out(dve.tensor_tensor(y[:, tt, :], hb[:, tt, :], ps[0:TT, 0:D], ALU.add), f"y{tt}")

                @block.gpsimd
                def _(pool):
                    chain = [0]

                    def link(ins):
                        chain[0] += 1
                        ins.then_inc(pool_chain, 1)
                        pool.wait_ge(pool_chain, chain[0])

                    def inverse_deviation(mv, var, var_ready, rstd, rstd_ready, eps, count):
                        pool.wait_ge(var_ready, count)
                        link(pool.tensor_scalar(var[:, :], mv[:, :, 1], eps, None, ALU.add))
                        pool.tensor_tensor(rstd[:, :], var[:, :], neg_half[:, :], ALU.pow).then_inc(rstd_ready, 1)

                    def front_step(n):
                        if n == 0:
                            inverse_deviation(f_mv, f_var, f_var_ready, f_rstd, f_rstd_ready, EPS, 1)
                        if n in (2, 4):
                            tt = (n - 2) // 2
                            pool.wait_ge(ssq_ready, 2 * tt + 2)
                            link(pool.tensor_tensor(ssum[:, :], ssq[:, 0:1], ssq[:, 1:2], ALU.add))
                            link(pool.tensor_scalar(smean[:, :], ssum[:, :], 1.0 / NTOK, None, ALU.mult))
                            pool.tensor_tensor(a_scale[:, tt:tt + 1], smean[:, :], neg_half[:, 0:1], ALU.pow)\
                                .then_inc(a_scale_ready, 1)
                        if n == 5:
                            inverse_deviation(f_mv, f_var, f_var_ready, f_rstd, f_rstd_ready, EPS, 2)

                    def lo_parts(st, tt):
                        pool.wait_ge(hi_ready, 2 * (2 * st + tt + 1))
                        pool.tensor_tensor(q_stack[:, :, 2, :], qk[:, tt, 0, :, :], q_stack[:, :, 0, :].bitcast(F32),
                                           ALU.subtract).then_inc(lo_ready, 1)
                        pool.tensor_tensor(k_stack[:, :, 1, :], qk[:, tt, 1, :, :], k_stack[:, :, 0, :].bitcast(F32),
                                           ALU.subtract).then_inc(lo_ready, 1)

                    def front_beside(st, phase):
                        for h in range(H):
                            for n in steps_at((st, phase, h)):
                                front_step(n)

                    if not B_ON:
                        for n in range(8):
                            front_step(n)
                        return
                    inverse_deviation(b_mv, b_var, b_var_ready, b_rstd, b_rstd_ready, EPS, 1)
                    lo_parts(0, 0)
                    lo_parts(0, 1)
                    front_beside(0, "scores")
                    front_beside(0, "attend")
                    inverse_deviation(b_mv, b_var, b_var_ready, b_rstd, b_rstd_ready, EPS, 2)
                    inverse_deviation(b_mv, b_var, b_var_ready, b_rstd, b_rstd_ready, EPS_MIX, 3)
                    lo_parts(1, 0)
                    lo_parts(1, 1)
                    lo_parts(2, 0)
                    front_beside(1, "scores")
                    lo_parts(2, 1)
                    front_beside(1, "attend")
                    inverse_deviation(b_mv, b_var, b_var_ready, b_rstd, b_rstd_ready, EPS_MIX, 4)

            nc.all_engine_barrier(sems_to_clear=per_iteration)

        iteration(0, None)
        with nc.Fori(0, B - 1) as clip:
            iteration(clip + 1, clip)
        iteration(None, B - 1)


def kernel(**inputs):
    import numpy as np
    import concourse.bacc as bacc
    from concourse.bass_utils import run_bass_kernel_spmd

    w = {name: np.asarray(a) for name, a in inputs.items()}

    def columns(a):
        return a.reshape(-1, 128, a.shape[-1]).transpose(1, 0, 2)

    mha = [[w[f"L1_ffn_mha_{n}"][m].reshape(D, H * HD) for n in ("wq", "wk", "wv")] for m in range(2)]
    qkv = [[w[f"L1_attn_{n}"].T for n in ("Wq", "Wk", "Wv")]] + mha
    arrays = {
        "x": w["x"],
        "conv_w": columns(w["L0_tok_W"].T),
        "conv_rows": np.stack([w["L0_tok_b"], w["L0_tok_gamma"], w["L0_tok_beta"],
                               w["L0_tok_running_mean"], w["L0_tok_running_var"]]),
        "keys": columns(w["L0_attn_key_param_tokens"].T),
        "values": columns(w["L0_attn_value_param_tokens"]),
        "route": columns(np.concatenate([w["L0_ffn_w_route"], w["L0_ffn_compress"]]).T),
        "routed": w["L0_ffn_routed"].transpose(0, 2, 1).reshape(E * R, D),
        "qkv_w": np.stack([columns(np.concatenate(s, axis=1)) for s in qkv], axis=1),
        "qkv_bias": np.stack([np.concatenate([w[f"L1_ffn_mha_{n}"][m].reshape(-1) for n in ("bq", "bk", "bv")])
                              for m in range(2)]),
        "wo": np.stack([columns(w["L1_ffn_mha_wo"][m].reshape(D, D)) for m in range(2)], axis=1),
        "bo": w["L1_ffn_mha_bo"],
        "ln_cols": np.stack([w[f"L1_ffn_{n}"].reshape(DK, 128).T for n in ("ln1_g", "ln1_b", "ln2_g", "ln2_b")], axis=1),
        "mix_rw": columns(w["L1_ffn_mha_rw"]),
        "mix_rb": w["L1_ffn_mha_rb"].reshape(1, -1),
        "ex_rw": columns(w["L1_ffn_ffn_rw"]),
        "ex_rb": w["L1_ffn_ffn_rb"].reshape(1, -1),
        "fw1": w["L1_ffn_fw1"].reshape(EX, DK, 128, F).transpose(2, 0, 1, 3).reshape(128, EX, DK * F),
        "fw2": w["L1_ffn_fw2"].reshape(EX, FK, 128, D).transpose(2, 0, 1, 3).reshape(128, EX, FK * D),
    }
    arrays = {name: np.ascontiguousarray(a) for name, a in arrays.items()}
    nc = bacc.Bacc("TRN2", target_bir_lowering=False, num_devices=1)
    inp = {name: nc.dram_tensor(f"in_{name}", shape, F32, kind="ExternalInput").ap() for name, shape in INPUTS.items()}
    out = nc.dram_tensor("out", [B, TP, D], F32, kind="ExternalOutput").ap()
    audio_tower(nc, inp, out)
    r = run_bass_kernel_spmd(nc, [{f"in_{name}": a for name, a in arrays.items()}], core_ids=[0])
    return r.results[0]["out"]
```

```python
from contextlib import ExitStack

import concourse.bass as bass
from concourse import mybir

F32 = mybir.dt.float32
F32R = mybir.dt.float32r
I32 = mybir.dt.int32
U32 = mybir.dt.uint32
ALU = mybir.AluOpType
ACT = mybir.ActivationFunctionType
AX = mybir.AxisListType

B, T, DIN = 32, 256, 128
CONTEXT = 5
TP = T - (CONTEXT - 1)
TT = TP // 2
D = 256
DK = D // 128
NTOK = 1024
NK = NTOK // 128
E, R = 8, 16
LORA_SCALE = 32.0 / R
H, HD = 16, 16
PAIRS = H // 2
SLOTS = 4
HW = SLOTS * HD
SETS = 3
SCALE = [1.0 / 16.0, 1.0 / 4.0, 1.0 / 4.0]
VW = 32
EX = 8
F = 2 * D
FK = F // 128
EPS = 1e-5
EPS_MIX = 1e-6
PT_RING = 8

INPUTS = {
    "x": [B, T, DIN], "conv_w": [128, CONTEXT, D], "conv_rows": [5, D],
    "keys": [128, DK, NTOK], "values": [128, NK, D], "route": [128, DK, E + R], "routed": [128, D],
    "qkv_w": [128, SETS, DK, 3 * D], "qkv_bias": [2, 3 * D], "wo": [128, 2, DK, D], "bo": [2, D],
    "ln_cols": [128, 4, DK], "mix_rw": [128, DK, 2], "mix_rb": [1, 2], "ex_rw": [128, DK, EX], "ex_rb": [1, EX],
    "fw1": [128, EX, DK * F], "fw2": [128, EX, FK * D],
}



def attention(scored, attended, beside, lag=0):
    for h in range(H + (lag if scored is not None else 0)):
        if attended is not None and h < H:
            yield "attend", attended, h
        if scored is not None and 0 <= h - lag < H:
            yield "score", scored, h - lag
        yield from beside.get(h, ())


def stages():
    yield "n4",
    yield "hb",
    yield "qk", 1, 0
    yield "split", 1, 0
    yield "x_columns",
    yield "qk", 1, 1
    yield "mean", 0
    yield "conv", 0
    yield "stack", 1, 0
    yield "split", 1, 1
    yield "conv", 1
    yield "logits", 0
    yield "batch_norm",
    yield "norm", 1
    yield "v", 1, 0
    yield "stack", 1, 1
    yield "rows", 1
    yield "mix_weights",
    yield "v", 1, 1
    yield from attention(1, None, {
        1: [("n1",)], 2: [("keys", 0, 0)], 3: [("keys", 0, 1)], 4: [("gelu", 0)], 5: [("qk", 2, 0)],
        6: [("split", 2, 0), ("gelu_columns", 0, 0)], 7: [("gelu_columns", 0, 1)],
        8: [("token_values", 0, 0)], 9: [("stack", 2, 0), ("qk", 2, 1)], 10: [("token_values", 0, 1), ("split", 2, 1)],
        11: [("keys", 1, 0)], 12: [("keys", 1, 1)], 13: [("stack", 2, 1), ("gelu", 1)], 14: [("bias_rows",)]})
    yield "max_split", 1
    yield "max_columns", 1
    yield "gelu_columns", 1, 0
    yield "gelu_columns", 1, 1
    yield "token_values", 1, 0
    yield "token_values", 1, 1
    yield from attention(2, 1, {
        0: [("norm", 2)], 1: [("rows", 2)], 2: [("n2",)], 3: [("route",)], 4: [("gates",)], 5: [("weigh", 1, 0)],
        6: [("ceg_columns",)], 8: [("ffn",)], 9: [("weigh", 1, 1), ("norm", 3)],
        10: [("rows", 3), ("context", 1, 0)], 11: [("n3",)], 12: [("qk", 0, 0)], 13: [("weigh", 1, 2), ("split", 0, 0)],
        14: [("qk", 0, 1)]})
    yield "weigh", 1, 3
    yield "max_split", 2
    yield "max_columns", 2
    yield "stack", 0, 0
    yield "v", 2, 0
    yield "split", 0, 1
    yield "v", 2, 1
    yield "context", 1, 1
    yield "stack", 0, 1
    yield "cT", 0
    yield from attention(0, 2, {
        2: [("wo", 0)], 5: [("weigh", 2, 0)], 9: [("weigh", 2, 1)], 11: [("context", 2, 0)], 13: [("weigh", 2, 2)]})
    yield "weigh", 2, 3
    yield "max_split", 0
    yield "max_columns", 0
    yield "v", 0, 0
    yield "context", 2, 1
    yield "v", 0, 1
    yield "cT", 1
    yield "wo", 1
    yield "norm", 6
    yield from attention(None, 0, {
        1: [("rows", 6)], 2: [("n5",)], 3: [("mean", 1)], 4: [("logits", 1)], 5: [("weigh", 0, 0)], 6: [("experts_chosen",)],
        9: [("weigh", 0, 1)], 10: [("hidden", 0, 0)], 11: [("context", 0, 0)], 12: [("hidden", 0, 1)],
        14: [("weigh", 0, 2)]})
    yield "hidden_columns", 0, 0
    yield "hidden", 1, 0
    yield "weigh", 0, 3
    yield "hidden_columns", 0, 1
    yield "hidden", 1, 1
    yield "context", 0, 1
    yield "expert_out", 0
    yield "norm", 4
    yield "hidden_columns", 1, 0
    yield "hidden_columns", 1, 1
    yield "rows", 4
    yield "norm", 5
    yield "expert_out", 1
    yield "rows", 5


STAGES = list(stages())
FRONT_STAGES = ("x_columns", "conv", "batch_norm", "n1", "keys", "gelu", "gelu_columns", "token_values",
                "n2", "route", "gates", "ceg_columns", "ffn", "n3")


def in_front(stage):
    name = stage[0]
    shared = ("qk", "v", "split", "stack", "score", "attend", "max_split", "max_columns", "weigh", "context")
    if name in ("norm", "rows"):
        return stage[1] != 6
    return name in FRONT_STAGES or name in shared and stage[1] == 0


def fills(stage):
    name, args = stage[0], "".join(str(a) for a in stage[1:])
    if name == "stack":
        return [f"t{w}{args}{half}" for w in "qk" for half in range(2)]
    if name == "conv":
        return ["conv"] if args == "1" else []
    if name == "token_values":
        return [f"av{args[0]}"] if args[1] == "1" else []
    return {"n1": ["n1T"], "n2": ["n2T"], "n3": ["n3T"], "n4": ["n4T"], "n5": ["n5T"], "x_columns": ["xT"],
            "keys": ["a" + args], "gelu_columns": ["gT" + args], "route": ["rc"], "ceg_columns": ["cegT"],
            "ffn": ["ffn"], "qk": ["qk" + args], "v": ["v" + args], "max_columns": ["mx" + args],
            "weigh": ["o" + args], "context": ["c" + args], "cT": ["cT" + args], "wo": ["wo" + args],
            "logits": ["lg" + args], "hidden": ["h" + args], "hidden_columns": ["hT" + args],
            "expert_out": ["y" + args]}.get(name, [])


FRONT_FILLS = [f for s in STAGES if in_front(s) for f in fills(s)]
BACK_FILLS = [f for s in STAGES if not in_front(s) for f in fills(s)]
TABLE = {1: 0, 2: 1, 0: 0}

LOADS = 10 + 2 * EX + 11


def audio_tower(nc, inp, out):
    with ExitStack() as ctx:
        def sb(name, shape, dt=F32):
            return ctx.enter_context(nc.sbuf_tensor(name, shape, dt))

        def psum(name):
            return ctx.enter_context(nc.psum_tensor(name, [128, 512], F32))

        def sem(name):
            return ctx.enter_context(nc.semaphore(name))

        conv_w = sb("conv_w", [128, CONTEXT, D])
        conv_b = sb("conv_b", [TT, D])
        bn_a = sb("bn_a", [TT, D])
        bn_b = sb("bn_b", [TT, D])
        keys = sb("keys", [128, DK, NTOK])
        values = sb("values", [128, NK, D])
        route = sb("route", [128, DK, E + R])
        routed = sb("routed", [128, D])
        qkv_w = sb("qkv_w", [128, SETS, DK, 3 * D])
        qkv_bias = sb("qkv_bias", [TT, 2, 3 * D])
        wo = sb("wo", [128, 2, DK, D])
        bo = sb("bo", [TT, 2, D])
        ln_cols = sb("ln_cols", [128, 4, DK])
        mix_rw = sb("mix_rw", [128, DK, 2])
        mix_rb = sb("mix_rb", [128, 2])
        ex_rw = sb("ex_rw", [128, DK, EX])
        ex_rb = sb("ex_rb", [128, EX])
        fw1 = sb("fw1", [128, EX * DK * F])
        fw2 = sb("fw2", [128, EX * FK * D])
        identr = sb("identr", [128, 128], F32R)
        ident = identr[:, :].bitcast(F32)
        iota_i = sb("iota_i", [TT, E], I32)
        iota = sb("iota", [TT, E])
        neg_half = sb("neg_half", [TT, 2])

        gel_room = sb("gel_room", [128, NTOK])
        xs = gel_room[:, 0:2 * DIN].rearrange("p (t d) -> p t d", t=2)
        xT = gel_room[:, 2 * DIN:2 * DIN + T]
        nf = gel_room[0:TT, 2 * D:4 * D].rearrange("p (t d) -> p t d", t=2)
        ceg = gel_room[0:TT, 0:2 * E * R].rearrange("p (t e r) -> p t e r", t=2, e=E)
        gel = gel_room[0:TT, :]
        cxT = gel_room[:, 0:2 * DK * TP].rearrange("p (m k t) -> p m k t", m=2, k=DK)
        hid = gel_room[0:TT, :].rearrange("p (e f) -> p e f", e=2)
        gelT = sb("gelT", [128, NK, TT])
        cegT = gelT[:, 0:2, :].rearrange("p k t -> p (k t)")
        hidT = gelT[:, :, :].rearrange("p (e c) t -> p e c t", e=2)
        hf = sb("hf", [TT, 2, D])
        nfT = sb("nfT", [128, DK, TP])
        f_stats = sb("f_stats", [TT, 2, 6])
        f_mv = sb("f_mv", [TT, 2, 2])
        f_var = sb("f_var", [TT, 2])
        f_rstd = sb("f_rstd", [TT, 2])
        ssq = sb("ssq", [TT, 2])
        ssum = sb("ssum", [TT, 1])
        smean = sb("smean", [TT, 1])
        a_scale = sb("a_scale", [TT, 2])
        rc = sb("rc", [TT, 2, E + R])
        top_v = sb("top_v", [TT, 2, 8])
        top_i = sb("top_i", [TT, 2, 8], U32)
        top_f = sb("top_f", [TT, 2, 8])
        gap = sb("gap", [TT, 2])
        gap_e = sb("gap_e", [TT, 2])
        gap_p = sb("gap_p", [TT, 2])
        w_first = sb("w_first", [TT, 2])
        w_second = sb("w_second", [TT, 2])
        gate = sb("gate", [TT, 2, E])
        gate2 = sb("gate2", [TT, 2, E])

        hb = sb("hb", [TT, 2, D])
        xm = sb("xm", [TT, 2, D])
        nb = sb("nb", [TT, 2, D])
        nbT = sb("nbT", [128, DK, TP])
        b_stats = sb("b_stats", [TT, 2, 6])
        b_mv = sb("b_mv", [TT, 2, 2])
        b_var = sb("b_var", [TT, 2])
        b_rstd = sb("b_rstd", [TT, 2])
        cx = nb[:, :, :]
        qk_room = sb("qk_room", [128, 2 * 2 * D])
        qk = qk_room[0:TT, :].rearrange("p (t w h d) -> p t w h d", t=2, w=2, h=H)
        vaug = sb("vaug", [TT, 2, H, VW])
        q_stack = sb("q_stack", [TT, H, SLOTS, HD], F32R)
        k_stack = sb("k_stack", [TT, H, SLOTS, HD], F32R)
        qT = [sb(f"qT{i}", [128, PAIRS, TP], F32R) for i in range(2)]
        kT = [sb(f"kT{i}", [128, PAIRS, TP], F32R) for i in range(2)]
        row_max = sb("row_max", [TT, 2, H])
        max_parts = sb("max_parts", [TT, 2, 2, 2, PAIRS], F32R)
        room = sb("room", [128, PT_RING * 2 * TP])
        probs = room[0:TT, :].rearrange("p (h k t) -> p h k t", h=PT_RING, k=2)
        maxT = room[0:32, (2 * PT_RING - 1) * TP:2 * PT_RING * TP]
        oT = sb("oT", [128, 2, TP])
        rec = sb("rec", [TT, 2, 8])
        msum = sb("msum", [128, DK])
        logit = sb("logit", [128, EX])
        neg_max = sb("neg_max", [128, 1])
        expo = sb("expo", [128, EX])
        esum = sb("esum", [128, 1])
        erec = sb("erec", [128, 1])
        mix_p = sb("mix_p", [128, 2])
        ex_p = sb("ex_p", [128, EX])
        ex_v = sb("ex_v", [128, 8])
        ex_i = sb("ex_i", [128, 8], U32)
        ex_o = sb("ex_o", [1, 8], I32)
        pair_sum = sb("pair_sum", [128, 1])
        pair_rec = sb("pair_rec", [128, 1])
        ex_w = sb("ex_w", [128, 2])
        y = hb[:, :, :]

        front_bank = [psum("front0"), psum("front1")]
        score_bank = [psum("score0"), psum("score1")]
        prob_bank = [psum("prob0"), psum("prob1")]
        back_bank = [psum("back0"), psum("back1")]

        loaded = sem("loaded")
        const_ready = sem("const_ready")
        front_full = [sem("front_full0"), sem("front_full1")]
        front_read = [sem("front_read0"), sem("front_read1")]
        back_full = [sem("back_full0"), sem("back_full1")]
        back_read = [sem("back_read0"), sem("back_read1")]
        x_loaded = sem("x_loaded")
        f_var_ready = sem("f_var_ready")
        f_rstd_ready = sem("f_rstd_ready")
        f_n_ready = sem("f_n_ready")
        ssq_ready = sem("ssq_ready")
        a_scale_ready = sem("a_scale_ready")
        gap_ready = sem("gap_ready")
        gap_exp_ready = sem("gap_exp_ready")
        ceg_ready = sem("ceg_ready")
        hb_copied = sem("hb_copied")
        b_var_ready = sem("b_var_ready")
        b_rstd_ready = sem("b_rstd_ready")
        b_n_ready = sem("b_n_ready")
        hi_ready = sem("hi_ready")
        lo_ready = sem("lo_ready")
        scores_full = sem("scores_full")
        maxima_done = sem("maxima_done")
        parts_ready = sem("parts_ready")
        max_placed = sem("max_placed")
        shifted_full = sem("shifted_full")
        exp_done = sem("exp_done")
        msum_ready = sem("msum_ready")
        logit_ready = sem("logit_ready")
        softexp_ready = sem("softexp_ready")
        expert_ready = sem("expert_ready")
        y_stored = sem("y_stored")
        act_chain = sem("act_chain")
        dve_chain = sem("dve_chain")
        pool_chain = sem("pool_chain")
        per_iteration = range(front_full[0].num, pool_chain.num + 1)

        FILL = {}
        for fills, banks, full, read in ((FRONT_FILLS, front_bank, front_full, front_read),
                                         (BACK_FILLS, back_bank, back_full, back_read)):
            for n, name in enumerate(fills):
                FILL[name] = (banks[n % 2], full[n % 2], read[n % 2], n // 2 + 1)

        def filled(eng, name):
            ps, full, _, n = FILL[name]
            eng.wait_ge(full, n)
            return ps

        def wait_read(eng, name):
            _, _, read, n = FILL[name]
            eng.wait_ge(read, n)

        def read_out(ins, name):
            ins.then_inc(FILL[name][2], 1)

        eye = oT[:, 0, 0:128]

        with nc.Block() as block:
            @block.sync
            def _(sp):
                for dst, name in ((conv_w, "conv_w"), (keys, "keys"), (values, "values"), (route, "route"),
                                  (routed, "routed"), (qkv_w, "qkv_w"), (wo, "wo"), (ln_cols, "ln_cols"),
                                  (mix_rw, "mix_rw"), (ex_rw, "ex_rw")):
                    shape = INPUTS[name]
                    full = (slice(None),) * len(shape)
                    sp.dma_start(dst[full], inp[name][full]).then_inc(loaded, 16)
                for e in range(EX):
                    sp.dma_start(fw1[:, e * DK * F:(e + 1) * DK * F], inp["fw1"][:, e, :]).then_inc(loaded, 16)
                    sp.dma_start(fw2[:, e * FK * D:(e + 1) * FK * D], inp["fw2"][:, e, :]).then_inc(loaded, 16)
                rows = [(conv_b[:, :], inp["conv_rows"][0:1, :]),
                        (hf[:, 0, :], inp["conv_rows"][1:2, :]), (hf[:, 1, :], inp["conv_rows"][2:3, :]),
                        (nf[:, 0, :], inp["conv_rows"][3:4, :]), (nf[:, 1, :], inp["conv_rows"][4:5, :]),
                        (mix_rb[:, :], inp["mix_rb"][0:1, :]), (ex_rb[:, :], inp["ex_rb"][0:1, :])]
                rows += [(qkv_bias[:, m, :], inp["qkv_bias"][m:m + 1, :]) for m in range(2)]
                rows += [(bo[:, m, :], inp["bo"][m:m + 1, :]) for m in range(2)]
                for dst, src in rows:
                    sp.dma_start(dst, src[0, :].partition_broadcast(dst.shape[0])).then_inc(loaded, 16)
                sp.wait_ge(loaded, 16 * LOADS)

            @block.gpsimd
            def _(pool):
                pool.memset(eye, 0.0).then_inc(const_ready, 1)
                pool.wait_ge(const_ready, 1)
                pool.affine_select(out=eye, in_=eye, compare_op=ALU.not_equal, fill=1.0, base=0,
                                   pattern=[[-1, 128]], channel_multiplier=1).then_inc(const_ready, 1)
                pool.iota(iota_i[:, :], pattern=[[1, E]], base=0, channel_multiplier=0).then_inc(const_ready, 1)
                pool.memset(neg_half[:, :], -0.5).then_inc(const_ready, 1)
                pool.memset(bn_a[:, :], -0.5).then_inc(const_ready, 1)
                pool.wait_ge(loaded, 16 * LOADS)
                pool.tensor_scalar(nf[:, 1, :], nf[:, 1, :], EPS, None, ALU.add).then_inc(pool_chain, 1)
                pool.wait_ge(pool_chain, 1)
                pool.wait_ge(const_ready, 5)
                pool.tensor_tensor(bn_a[:, :], nf[:, 1, :], bn_a[:, :], ALU.pow).then_inc(pool_chain, 1)
                pool.wait_ge(pool_chain, 2)
                pool.tensor_tensor(bn_a[:, :], bn_a[:, :], hf[:, 0, :], ALU.mult).then_inc(pool_chain, 1)
                pool.wait_ge(pool_chain, 3)
                pool.tensor_tensor(nf[:, 0, :], nf[:, 0, :], bn_a[:, :], ALU.mult).then_inc(pool_chain, 1)
                pool.wait_ge(pool_chain, 4)
                pool.tensor_tensor(bn_b[:, :], hf[:, 1, :], nf[:, 0, :], ALU.subtract).then_inc(pool_chain, 1)

            @block.vector
            def _(dve):
                dve.wait_ge(const_ready, 3)
                dve.tensor_copy(identr[:, :], eye)
                dve.tensor_copy(iota[:, :], iota_i[:, :])
                dve.memset(q_stack[:, :, 3, :].bitcast(F32), 0.0)
                dve.memset(k_stack[:, :, 3, 2:HD].bitcast(F32), 0.0)
                dve.memset(k_stack[:, :, 3, 0:2].bitcast(F32), -1.0)
                dve.memset(vaug[:, :, :, HD:VW], 1.0)

        nc.all_engine_barrier(sems_to_clear=per_iteration)

        def iteration(front, back, stored):
            F_ON, B_ON = front is not None, back is not None
            SEQ = [1] * B_ON + [2] * B_ON + [0] * F_ON
            POS = {st: n for n, st in enumerate(SEQ)}

            def before(st):
                return SEQ[POS[st] - 1] if POS[st] else None

            def walk(parts):
                for stage in STAGES:
                    if (F_ON if in_front(stage) else B_ON) and stage[0] in parts:
                        parts[stage[0]](*stage[1:])

            NORM = {1: (hf, nf, EPS, 1), 2: (hf, nf, EPS, 2), 3: (hf, nf, EPS, 3), 4: (hf, xm, EPS, 4),
                    5: (xm, nb, EPS_MIX, 5), 6: (xm, nb, EPS_MIX, 1)}
            FRONT_NORM = (f_stats, f_mv, f_var, f_var_ready, f_rstd, f_rstd_ready, f_n_ready)
            BACK_NORM = (b_stats, b_mv, b_var, b_var_ready, b_rstd, b_rstd_ready, b_n_ready)

            with nc.Block(no_gpsimd_drain=True) as block:
                @block.sync
                def _(sp):
                    if F_ON:
                        sp.dma_start(xs, inp["x"][front, :, :].rearrange("(t p) d -> p t d", p=128))\
                          .then_inc(x_loaded, 16)
                    if stored is not None:
                        sp.dma_start(out[stored, :, :].rearrange("(t p) d -> p t d", p=TT), y)\
                          .then_inc(y_stored, 16)
                    for st in SEQ:
                        wait_read(sp, f"mx{st}")
                        for j in range(2):
                            for part in range(2):
                                r = 8 * (2 * j + part)
                                row = HW * j + 3 * HD + part
                                sp.dma_start(qT[TABLE[st]][row:row + 1, :, :].bitcast(F32), maxT[r:r + 8, :])\
                                  .then_inc(max_placed, 16)
                    if F_ON:
                        sp.wait_ge(x_loaded, 16)
                    if stored is not None:
                        sp.wait_ge(y_stored, 16)

                @block.tensor
                def _(pe):
                    chosen = []

                    def take(name):
                        ps, _, read, n = FILL[name]
                        if n > 1:
                            pe.wait_ge(read, n - 1)
                        return ps

                    def done(name, ins):
                        ins.then_inc(FILL[name][1], 1)

                    def turn(name, src):
                        ps = take(name)
                        for tt in range(2):
                            for k in range(DK):
                                c = k * TP + tt * TT
                                last = pe.transpose(ps[:, c:c + TT], src[:, tt, k * 128:(k + 1) * 128],
                                                    ident[0:TT, 0:TT])
                        done(name, last)

                    def x_columns():
                        pe.wait_ge(x_loaded, 16)
                        ps = take("xT")
                        for t in range(2):
                            last = pe.transpose(ps[:, t * 128:(t + 1) * 128], xs[:, t, :], ident)
                        done("xT", last)

                    def conv(tt):
                        ps = FILL["conv"][0]
                        if tt == 0:
                            take("conv")
                            wait_read(pe, "xT")
                        for c in range(CONTEXT):
                            last = pe.matmul(ps[0:TT, tt * D:(tt + 1) * D], xT[:, tt * TT + c:tt * TT + c + TT],
                                             conv_w[:, c, :], start=c == 0, stop=c == CONTEXT - 1)
                        if tt:
                            done("conv", last)

                    def n1():
                        pe.wait_ge(f_n_ready, 1)
                        turn("n1T", nf)

                    def n2():
                        pe.wait_ge(f_n_ready, 2)
                        turn("n2T", nf)

                    def n3():
                        pe.wait_ge(f_n_ready, 3)
                        turn("n3T", nf)

                    def n4():
                        turn("n4T", nb)

                    def n5():
                        pe.wait_ge(b_n_ready, 1)
                        turn("n5T", nb)

                    def keys_(tt, half):
                        if (tt, half) == (0, 0):
                            wait_read(pe, "n1T")
                        name = f"a{tt}{half}"
                        ps = take(name)
                        for k in range(DK):
                            last = pe.matmul(ps[0:TT, :], nfT[:, k, tt * TT:(tt + 1) * TT],
                                             keys[:, k, half * 512:(half + 1) * 512], start=k == 0, stop=k == DK - 1)
                        done(name, last)

                    def gelu_columns(tt, half):
                        wait_read(pe, f"a{tt}{half}")
                        name = f"gT{tt}{half}"
                        ps = take(name)
                        for c in range(4):
                            blk = 4 * half + c
                            last = pe.transpose(ps[:, c * TT:(c + 1) * TT], gel[:, blk * 128:(blk + 1) * 128],
                                                ident[0:TT, 0:TT])
                        done(name, last)

                    def token_values(tt, half):
                        name = f"av{tt}"
                        ps = take(name) if half == 0 else FILL[name][0]
                        wait_read(pe, f"gT{tt}{half}")
                        for blk in range(4 * half, 4 * half + 4):
                            last = pe.matmul(ps[0:TT, 0:D], gelT[:, blk, :], values[:, blk, :],
                                             start=blk == 0, stop=blk == NK - 1)
                        if half:
                            done(name, last)

                    def route_():
                        ps = take("rc")
                        wait_read(pe, "n2T")
                        for tt in range(2):
                            for k in range(DK):
                                last = pe.matmul(ps[0:TT, tt * 32:tt * 32 + E + R], nfT[:, k, tt * TT:(tt + 1) * TT],
                                                 route[:, k, :], start=k == 0, stop=k == DK - 1)
                        done("rc", last)

                    def ceg_columns():
                        pe.wait_ge(ceg_ready, 1)
                        ps = take("cegT")
                        for tt in range(2):
                            last = pe.transpose(ps[:, tt * TT:(tt + 1) * TT],
                                                ceg[:, tt, :, :].rearrange("p e r -> p (e r)"), ident[0:TT, 0:TT])
                        done("cegT", last)

                    def ffn():
                        ps = take("ffn")
                        wait_read(pe, "cegT")
                        for tt in range(2):
                            last = pe.matmul(ps[0:TT, tt * D:(tt + 1) * D], cegT[:, tt * TT:(tt + 1) * TT],
                                             routed[:, :], start=True, stop=True)
                        done("ffn", last)

                    def project(what, st, tt, lo, hi):
                        src = nbT if st else nfT
                        ps = take(f"{what}{st}{tt}")
                        for k in range(DK):
                            last = pe.matmul(ps[0:TT, 0:hi - lo], src[:, k, tt * TT:(tt + 1) * TT],
                                             qkv_w[:, st, k, lo:hi], start=k == 0, stop=k == DK - 1)
                        done(f"{what}{st}{tt}", last)

                    def qk_(st, tt):
                        wait_read(pe, "n4T" if st else "n3T")
                        project("qk", st, tt, 0, 2 * D)

                    def v(st, tt):
                        project("v", st, tt, 2 * D, 3 * D)

                    def stack(st, tt):
                        n = 2 * (2 * POS[st] + tt + 1)
                        pe.wait_ge(hi_ready, n)
                        pe.wait_ge(lo_ready, n)
                        for w, src in (("q", q_stack), ("k", k_stack)):
                            for half in range(2):
                                name = f"t{w}{st}{tt}{half}"
                                ps = take(name)
                                for c in range(4):
                                    p = 4 * half + c
                                    last = pe.transpose(ps[:, c * TT:(c + 1) * TT].bitcast(F32R),
                                                        src[:, 2 * p:2 * p + 2, :, :].rearrange("q h s d -> q (h s d)"),
                                                        identr[0:TT, 0:TT])
                                done(name, last)

                    def score(st, h):
                        n = H * POS[st] + h
                        if h == 0:
                            for tt in range(2):
                                for w in "qk":
                                    for half in range(2):
                                        wait_read(pe, f"t{w}{st}{tt}{half}")
                        if n >= 2:
                            pe.wait_ge(maxima_done, n - 1)
                        p, r = h // 2, HW * (h % 2)
                        for tt in range(2):
                            last = pe.matmul(score_bank[n % 2][0:TT, tt * TP:(tt + 1) * TP],
                                             qT[TABLE[st]][r:r + HW, p, tt * TT:(tt + 1) * TT],
                                             kT[TABLE[st]][r:r + HW, p, :], start=True, stop=True)
                        last.then_inc(scores_full, 1)

                    def max_columns(st):
                        pe.wait_ge(parts_ready, POS[st] + 1)
                        ps = take(f"mx{st}")
                        for tt in range(2):
                            last = pe.transpose(ps[0:32, tt * TT:(tt + 1) * TT].bitcast(F32R),
                                                max_parts[:, tt, :, :, :].rearrange("q j s p -> q (j s p)"),
                                                identr[0:TT, 0:TT])
                        done(f"mx{st}", last)

                    def attend(st, h):
                        n = H * POS[st] + h
                        if h == 0:
                            pe.wait_ge(max_placed, 64 * (POS[st] + 1))
                        if n >= 2:
                            pe.wait_ge(exp_done, n - 1)
                        p, r = h // 2, HW * (h % 2)
                        for tt in range(2):
                            last = pe.matmul(prob_bank[n % 2][0:TT, tt * TP:(tt + 1) * TP],
                                             kT[TABLE[st]][r:r + HW, p, tt * TT:(tt + 1) * TT],
                                             qT[TABLE[st]][r:r + HW, p, :], start=True, stop=True)
                        last.then_inc(shifted_full, 1)

                    def weigh(st, g):
                        pe.wait_ge(exp_done, H * POS[st] + 4 * g + 4)
                        if g == 0:
                            wait_read(pe, f"v{st}0")
                            wait_read(pe, f"v{st}1")
                        ps = take(f"o{st}{g}")
                        for tt in range(2):
                            for c in range(4):
                                h = 4 * g + c
                                last = pe.matmul(ps[32 * c:32 * c + 32, 0:TP], vaug[:, tt, h, :],
                                                 probs[:, h % PT_RING, tt, :], start=tt == 0, stop=tt == 1,
                                                 skip_group_check=True)
                        done(f"o{st}{g}", last)

                    def context(st, gg):
                        wait_read(pe, f"o{st}{2 * gg}")
                        wait_read(pe, f"o{st}{2 * gg + 1}")
                        ps = take(f"c{st}{gg}")
                        for g in range(2):
                            for tt in range(2):
                                c = (2 * tt + g) * 128
                                last = pe.transpose(ps[0:TT, c:c + 128], oT[:, g, tt * TT:(tt + 1) * TT], ident)
                        done(f"c{st}{gg}", last)

                    def logits(i):
                        w, n = ((mix_rw, 2), (ex_rw, EX))[i]
                        pe.wait_ge(msum_ready, i + 1)
                        ps = take(f"lg{i}")
                        for k in range(DK):
                            last = pe.matmul(ps[:, 0:n], msum[:, k:k + 1].broadcast_to([128, 128]), w[:, k, :],
                                             start=k == 0, stop=k == DK - 1)
                        done(f"lg{i}", last)

                    def cT(m):
                        wait_read(pe, f"c{m + 1}0")
                        wait_read(pe, f"c{m + 1}1")
                        turn(f"cT{m}", cx)

                    def wo_(m):
                        ps = take(f"wo{m}")
                        wait_read(pe, f"cT{m}")
                        for tt in range(2):
                            for k in range(DK):
                                last = pe.matmul(ps[0:TT, tt * D:(tt + 1) * D], cxT[:, m, k, tt * TT:(tt + 1) * TT],
                                                 wo[:, m, k, :], start=k == 0, stop=k == DK - 1)
                        done(f"wo{m}", last)

                    def hidden(tt, k):
                        if (tt, k) == (0, 0):
                            pe.wait_ge(expert_ready, 1)
                            chosen.extend(pe.value_load(ex_o[0:1, i:i + 1], min_val=0, max_val=EX - 1)
                                          for i in range(2))
                        ps = take(f"h{tt}{k}")
                        for d in range(DK):
                            last = pe.matmul(ps[0:TT, :], nbT[:, d, tt * TT:(tt + 1) * TT],
                                             fw1[:, bass.ds(chosen[k] * (DK * F) + d * F, F)],
                                             start=d == 0, stop=d == DK - 1)
                        done(f"h{tt}{k}", last)

                    def hidden_columns(tt, k):
                        wait_read(pe, f"h{tt}{k}")
                        ps = take(f"hT{tt}{k}")
                        for c in range(FK):
                            last = pe.transpose(ps[:, c * TT:(c + 1) * TT], hid[:, k, c * 128:(c + 1) * 128],
                                                ident[0:TT, 0:TT])
                        done(f"hT{tt}{k}", last)

                    def expert_out(tt):
                        ps = take(f"y{tt}")
                        for k in range(2):
                            wait_read(pe, f"hT{tt}{k}")
                            for c in range(FK):
                                last = pe.matmul(ps[0:TT, 0:D], hidT[:, k, c, :],
                                                 fw2[:, bass.ds(chosen[k] * (FK * D) + c * D, D)],
                                                 start=k + c == 0, stop=k + c == FK)
                        done(f"y{tt}", last)

                    walk({"x_columns": x_columns, "conv": conv, "n1": n1, "n2": n2, "n3": n3, "n4": n4, "n5": n5,
                          "keys": keys_, "gelu_columns": gelu_columns, "token_values": token_values, "route": route_,
                          "ceg_columns": ceg_columns, "ffn": ffn, "qk": qk_, "v": v, "stack": stack, "score": score,
                          "max_columns": max_columns, "attend": attend, "weigh": weigh, "context": context,
                          "logits": logits, "cT": cT, "wo": wo_, "hidden": hidden, "hidden_columns": hidden_columns,
                          "expert_out": expert_out})

                @block.scalar
                def _(act):
                    def columns(name, dst):
                        ps = filled(act, name)
                        read_out(act.copy(dst, ps[:, 0:DK * TP].rearrange("p (k t) -> p k t", k=DK)), name)

                    def gained_columns(name, i):
                        ps = filled(act, name)
                        for k in range(DK):
                            last = act.activation(nbT[:, k, :], ps[:, k * TP:(k + 1) * TP], ACT.Identity,
                                                  scale=ln_cols[:, i, k:k + 1], bias=ln_cols[:, i + 1, k:k + 1])
                        read_out(last, name)

                    def x_columns():
                        ps = filled(act, "xT")
                        read_out(act.copy(xT, ps[:, 0:T]), "xT")

                    def n1():
                        columns("n1T", nfT[:, :, :])

                    def n2():
                        columns("n2T", nfT[:, :, :])

                    def n3():
                        columns("n3T", nfT[:, :, :])

                    def n4():
                        gained_columns("n4T", 0)

                    def n5():
                        gained_columns("n5T", 2)

                    def hb_():
                        if stored is not None:
                            act.wait_ge(y_stored, 16)
                        act.copy(hb[:, :, :], hf[:, :, :]).then_inc(hb_copied, 1)

                    def keys_(tt, half):
                        if (tt, half) == (1, 0):
                            filled(act, "gT00")
                            filled(act, "gT01")
                        ps = filled(act, f"a{tt}{half}")
                        act.activation(gel[:, half * 512:(half + 1) * 512], ps[0:TT, :], ACT.Square,
                                       accum_out=ssq[:, half:half + 1]).then_inc(ssq_ready, 1)

                    def gelu(tt):
                        act.wait_ge(ssq_ready, 2 * tt + 2)
                        act.wait_ge(a_scale_ready, tt + 1)
                        for half in range(2):
                            ps = FILL[f"a{tt}{half}"][0]
                            read_out(act.activation(gel[:, half * 512:(half + 1) * 512], ps[0:TT, :], ACT.Gelu,
                                                    scale=a_scale[:, tt:tt + 1]), f"a{tt}{half}")

                    def route_():
                        act.wait_ge(gap_ready, 1)
                        act.activation(gap_e[:, :], gap[:, :], ACT.Exp).then_inc(gap_exp_ready, 1)

                    def ceg_columns():
                        ps = filled(act, "cegT")
                        read_out(act.copy(cegT[:, :], ps[:, 0:TP]), "cegT")

                    def qk_(st, tt):
                        if st == 0:
                            ps = filled(act, f"qk0{tt}")
                            if POS[0]:
                                act.wait_ge(lo_ready, 2 * (2 * (POS[0] - 1) + tt + 1))
                            read_out(act.copy(qk[:, tt, :, :, :].rearrange("p w h d -> p (w h d)"), ps[0:TT, :]),
                                     f"qk0{tt}")

                    def split(st, tt):
                        wait_read(act, f"qk{st}{tt}")
                        last = (st, 0) if tt else (before(st), 1)
                        if last[0] is not None:
                            filled(act, f"tq{last[0]}{last[1]}1")
                            filled(act, f"tk{last[0]}{last[1]}1")
                        act.copy(q_stack[:, :, 0:2, :],
                                 qk[:, tt, 0, :, :].unsqueeze(2).broadcast_to([TT, H, 2, HD])).then_inc(hi_ready, 1)
                        act.copy(k_stack[:, :, 0:3:2, :],
                                 qk[:, tt, 1, :, :].unsqueeze(2).broadcast_to([TT, H, 2, HD])).then_inc(hi_ready, 1)

                    def stack(st, tt):
                        if tt == 0 and st == 0 and B_ON:
                            act.wait_ge(exp_done, H)
                        for half in range(2):
                            name = f"tq{st}{tt}{half}"
                            ps = filled(act, name)
                            read_out(act.copy(qT[TABLE[st]][:, 4 * half:4 * half + 4, tt * TT:(tt + 1) * TT],
                                              ps[:, 0:4 * TT].rearrange("p (c t) -> p c t", c=4)), name)

                    def max_columns(st):
                        ps = filled(act, f"mx{st}")
                        if before(st) is not None:
                            act.wait_ge(max_placed, 64 * POS[st])
                            filled(act, f"o{before(st)}3")
                        read_out(act.copy(maxT, ps[0:32, 0:TP]), f"mx{st}")

                    def attend(st, h):
                        n = H * POS[st] + h
                        act.wait_ge(shifted_full, n + 1)
                        if n % 4 == 0 and n >= PT_RING:
                            g = n // 4 - 2
                            filled(act, f"o{SEQ[g // 4]}{g % 4}")
                        act.activation(probs[:, h % PT_RING, :, :],
                                       prob_bank[n % 2][0:TT, 0:2 * TP].rearrange("p (k t) -> p k t", k=2),
                                       ACT.Exp, scale=SCALE[st]).then_inc(exp_done, 1)

                    def weigh(st, g):
                        if st == 0:
                            return
                        ps = filled(act, f"o{st}{g}")
                        if g >= 2:
                            filled(act, f"c{st}0")
                        elif before(st) is not None:
                            filled(act, f"c{before(st)}1")
                        read_out(act.copy(oT[:, g % 2, :], ps[:, 0:TP]), f"o{st}{g}")

                    def logits(i):
                        n = (2, EX)[i]
                        act.wait_ge(logit_ready, i + 1)
                        act.activation(expo[:, 0:n], logit[:, 0:n], ACT.Exp, bias=neg_max[:, :],
                                       accum_out=esum[:, :]).then_inc(softexp_ready, 1)

                    def cT(m):
                        columns(f"cT{m}", cxT[:, m, :, :])

                    def hidden(tt, k):
                        ps = filled(act, f"h{tt}{k}")
                        if tt:
                            filled(act, f"hT0{k}")
                        read_out(act.activation(hid[:, k, :], ps[0:TT, :], ACT.Gelu), f"h{tt}{k}")

                    walk({"x_columns": x_columns, "n1": n1, "n2": n2, "n3": n3, "n4": n4, "n5": n5, "hb": hb_,
                          "keys": keys_, "gelu": gelu, "route": route_, "ceg_columns": ceg_columns, "qk": qk_,
                          "split": split, "stack": stack, "max_columns": max_columns, "attend": attend,
                          "weigh": weigh, "logits": logits, "cT": cT, "hidden": hidden})

                @block.vector
                def _(dve):
                    chain = [0]

                    def link(ins):
                        chain[0] += 1
                        ins.then_inc(dve_chain, 1)
                        dve.wait_ge(dve_chain, chain[0])

                    def norm(i):
                        h = NORM[i][0]
                        stats, mv, _, var_ready, _, _, _ = BACK_NORM if i == 6 else FRONT_NORM
                        if i == 3:
                            wait_read(dve, "ffn")
                        if i == 4:
                            wait_read(dve, "c00")
                            wait_read(dve, "c01")
                            link(dve.tensor_tensor(hf[:, :, :], hf[:, :, :], cx[:, :, :], ALU.add))
                        if i == 5:
                            dve.wait_ge(f_n_ready, 4)
                        if i == 6:
                            wait_read(dve, "wo1")
                        for tt in range(2):
                            last = dve.bn_stats(stats[:, tt, :], h[:, tt, :])
                        link(last)
                        for tt in range(2):
                            last = dve.bn_aggr(mv[:, tt, :], stats[:, tt, :])
                        last.then_inc(var_ready, 1)
                        if i == 6:
                            dve.wait_ge(hb_copied, 1)
                            link(dve.tensor_tensor(hb[:, :, :], hb[:, :, :], xm[:, :, :], ALU.add))

                    def rows(i):
                        h, n, _, count = NORM[i]
                        _, mv, _, var_ready, rstd, rstd_ready, n_ready = BACK_NORM if i == 6 else FRONT_NORM
                        dve.wait_ge(var_ready, count)
                        dve.wait_ge(rstd_ready, count)
                        for tt in range(2):
                            last = dve.tensor_scalar(n[:, tt, :], h[:, tt, :], mv[:, tt, 0:1], rstd[:, tt:tt + 1],
                                                     ALU.subtract, ALU.mult)
                        last.then_inc(n_ready, 1)

                    def both(row):
                        return row.unsqueeze(1).broadcast_to([TT, 2, D])

                    def batch_norm():
                        ps = filled(dve, "conv")
                        if B_ON:
                            dve.wait_ge(hb_copied, 1)
                        read_out(dve.tensor_tensor(hf[:, :, :], ps[0:TT, :].rearrange("p (t d) -> p t d", t=2),
                                                   both(conv_b[:, :]), ALU.add), "conv")
                        wait_read(dve, "conv")
                        link(dve.scalar_tensor_tensor(hf[:, :, :], hf[:, :, :], 0.0, both(bn_a[:, :]),
                                                      ALU.max, ALU.mult))
                        link(dve.tensor_tensor(hf[:, :, :], hf[:, :, :], both(bn_b[:, :]), ALU.add))

                    def gelu_columns(tt, half):
                        if tt:
                            filled(dve, "av0")
                        ps = filled(dve, f"gT{tt}{half}")
                        read_out(dve.tensor_copy(gelT[:, 4 * half:4 * half + 4, :],
                                                 ps[:, 0:4 * TT].rearrange("p (c t) -> p c t", c=4)), f"gT{tt}{half}")

                    def token_values(tt, half):
                        if half:
                            ps = filled(dve, f"av{tt}")
                            read_out(dve.tensor_tensor(hf[:, tt, :], hf[:, tt, :], ps[0:TT, 0:D], ALU.add), f"av{tt}")
                            if tt:
                                wait_read(dve, "av0")
                                wait_read(dve, "av1")

                    def route_():
                        ps = filled(dve, "rc")
                        read_out(dve.tensor_copy(rc[:, :, :], ps[0:TT, 0:64].rearrange("p (t c) -> p t c", t=2)
                                                 [:, :, 0:E + R]), "rc")
                        wait_read(dve, "rc")
                        for tt in range(2):
                            last = dve.max(top_v[:, tt, :], rc[:, tt, 0:E])
                        link(last)
                        dve.tensor_tensor(gap[:, :], top_v[:, :, 1], top_v[:, :, 0], ALU.subtract)\
                           .then_inc(gap_ready, 1)
                        for tt in range(2):
                            last = dve.max_index(top_i[:, tt, :], top_v[:, tt, :], rc[:, tt, 0:E])
                        link(last)
                        link(dve.tensor_copy(top_f[:, :, :], top_i[:, :, :]))

                    def gates():
                        dve.wait_ge(gap_exp_ready, 1)
                        link(dve.tensor_scalar(gap_p[:, :], gap_e[:, :], 1.0, None, ALU.add))
                        link(dve.reciprocal(w_first[:, :], gap_p[:, :]))
                        link(dve.tensor_tensor(w_second[:, :], gap_e[:, :], w_first[:, :], ALU.mult))
                        for tt in range(2):
                            dve.tensor_scalar(gate[:, tt, :], iota[:, :], top_f[:, tt, 0:1], w_first[:, tt:tt + 1],
                                              ALU.is_equal, ALU.mult)
                            last = dve.tensor_scalar(gate2[:, tt, :], iota[:, :], top_f[:, tt, 1:2],
                                                     w_second[:, tt:tt + 1], ALU.is_equal, ALU.mult)
                        link(last)
                        link(dve.tensor_tensor(gate[:, :, :], gate[:, :, :], gate2[:, :, :], ALU.add))
                        dve.tensor_tensor(ceg[:, :, :, :], gate[:, :, :].unsqueeze(3).broadcast_to([TT, 2, E, R]),
                                          rc[:, :, E:E + R].unsqueeze(2).broadcast_to([TT, 2, E, R]),
                                          ALU.mult).then_inc(ceg_ready, 1)

                    def ffn():
                        ps = filled(dve, "ffn")
                        read_out(dve.scalar_tensor_tensor(hf[:, :, :], ps[0:TT, :].rearrange("p (t d) -> p t d", t=2),
                                                          LORA_SCALE, hf[:, :, :], ALU.mult, ALU.add), "ffn")

                    def stack(st, tt):
                        if tt == 0 and st == 0 and B_ON:
                            dve.wait_ge(exp_done, H)
                        for half in range(2):
                            name = f"tk{st}{tt}{half}"
                            ps = filled(dve, name)
                            read_out(dve.tensor_copy(kT[TABLE[st]][:, 4 * half:4 * half + 4, tt * TT:(tt + 1) * TT],
                                                     ps[:, 0:4 * TT].rearrange("p (c t) -> p c t", c=4)), name)

                    def v(st, tt):
                        name = f"v{st}{tt}"
                        ps = filled(dve, name)
                        if before(st) is not None:
                            filled(dve, f"o{before(st)}3")
                        src = ps[0:TT, 0:D].rearrange("p (h d) -> p h d", h=H)
                        dst = vaug[:, tt, :, 0:HD]
                        if st == 0:
                            read_out(dve.tensor_copy(dst, src), name)
                        else:
                            bias = qkv_bias[:, st - 1, 2 * D:3 * D].rearrange("p (h d) -> p h d", h=H)
                            read_out(dve.tensor_tensor(dst, src, bias, ALU.add), name)

                    def qk_(st, tt):
                        if st:
                            name = f"qk{st}{tt}"
                            ps = filled(dve, name)
                            if before(st) is not None:
                                dve.wait_ge(lo_ready, 2 * (2 * (POS[st] - 1) + tt + 1))
                            read_out(dve.tensor_tensor(qk[:, tt, :, :, :].rearrange("p w h d -> p (w h d)"), ps[0:TT, :],
                                                       qkv_bias[:, st - 1, 0:2 * D], ALU.add), name)

                    def score(st, h):
                        n = H * POS[st] + h
                        if h == 0 and before(st) is not None:
                            dve.wait_ge(parts_ready, POS[st])
                        dve.wait_ge(scores_full, n + 1)
                        dve.tensor_reduce(row_max[:, :, h], score_bank[n % 2][0:TT, 0:2 * TP]
                                          .rearrange("p (t k) -> p t k", t=2), AX.X, ALU.max).then_inc(maxima_done, 1)

                    def max_split(st):
                        dve.wait_ge(maxima_done, H * (POS[st] + 1))
                        if before(st) is not None:
                            filled(dve, f"mx{before(st)}")
                        src = row_max[:, :, :].rearrange("q t (p j) -> q t j p", j=2)
                        link(dve.tensor_copy(max_parts[:, :, :, 0, :], src))
                        dve.tensor_tensor(max_parts[:, :, :, 1, :], src, max_parts[:, :, :, 0, :].bitcast(F32),
                                          ALU.subtract).then_inc(parts_ready, 1)

                    def weigh(st, g):
                        if st:
                            return
                        ps = filled(dve, f"o{st}{g}")
                        if g >= 2:
                            filled(dve, f"c{st}0")
                        elif before(st) is not None:
                            filled(dve, f"c{before(st)}1")
                        read_out(dve.tensor_copy(oT[:, g % 2, :], ps[:, 0:TP]), f"o{st}{g}")

                    def context(st, gg):
                        name = f"c{st}{gg}"
                        ps = filled(dve, name)
                        src = ps[0:TT, :].rearrange("p (t h w) -> p t h w", t=2, w=VW)
                        link(dve.reciprocal(rec[:, :, :], src[:, :, :, HD]))
                        if st:
                            link(dve.tensor_scalar(rec[:, :, :], rec[:, :, :], mix_p[0:TT, st - 1:st], None, ALU.mult))
                        if gg == 0:
                            if st == 2:
                                filled(dve, "cT0")
                            if st == 0 and B_ON:
                                filled(dve, "n5T")
                        dst = cx[:, :, :].rearrange("p t (h d) -> p t h d", d=HD)[:, :, 8 * gg:8 * gg + 8, :]
                        read_out(dve.tensor_tensor(dst, src[:, :, :, 0:HD],
                                                   rec[:, :, :].unsqueeze(3).broadcast_to([TT, 2, 8, HD]),
                                                   ALU.mult), name)

                    def mean(i):
                        wait_read(dve, ("n4T", "n5T")[i])
                        dve.tensor_reduce(msum[:, :], nbT[:, :, :], AX.X, ALU.add).then_inc(msum_ready, 1)

                    def logits(i):
                        n, bias = ((2, mix_rb), (EX, ex_rb))[i]
                        name = f"lg{i}"
                        ps = filled(dve, name)
                        read_out(dve.scalar_tensor_tensor(logit[:, 0:n], ps[:, 0:n], 1.0 / TP, bias[:, 0:n],
                                                          ALU.mult, ALU.add), name)
                        wait_read(dve, name)
                        dve.tensor_reduce(neg_max[:, :], logit[:, 0:n], AX.X, ALU.max, negate=True)\
                           .then_inc(logit_ready, 1)

                    def probabilities(i, n, p):
                        dve.wait_ge(softexp_ready, i + 1)
                        link(dve.reciprocal(erec[:, :], esum[:, :]))
                        link(dve.tensor_scalar(p[:, 0:n], expo[:, 0:n], erec[:, 0:1], None, ALU.mult))

                    def mix_weights():
                        probabilities(0, 2, mix_p)

                    def bias_rows():
                        for m in range(2):
                            link(dve.scalar_tensor_tensor(xm[:, :, :], both(bo[:, m, :]), mix_p[0:TT, m:m + 1],
                                                          xm[:, :, :], ALU.mult, ALU.add))

                    def wo_(m):
                        name = f"wo{m}"
                        ps = filled(dve, name)
                        if m:
                            wait_read(dve, "wo0")
                        read_out(dve.tensor_tensor(xm[:, :, :], xm[:, :, :],
                                                   ps[0:TT, :].rearrange("p (t d) -> p t d", t=2), ALU.add), name)

                    def experts_chosen():
                        probabilities(1, EX, ex_p)
                        link(dve.max(ex_v[:, :], ex_p[:, :]))
                        link(dve.max_index(ex_i[:, :], ex_v[:, :], ex_p[:, :]))
                        dve.tensor_copy(ex_o[:, :], ex_i[0:1, :]).then_inc(expert_ready, 1)
                        link(dve.tensor_tensor(pair_sum[:, :], ex_v[:, 0:1], ex_v[:, 1:2], ALU.add))
                        link(dve.reciprocal(pair_rec[:, :], pair_sum[:, :]))
                        link(dve.tensor_scalar(ex_w[:, :], ex_v[:, 0:2], pair_rec[:, 0:1], None, ALU.mult))

                    def hidden_columns(tt, k):
                        name = f"hT{tt}{k}"
                        ps = filled(dve, name)
                        if tt:
                            filled(dve, "y0")
                        read_out(dve.tensor_scalar(hidT[:, k, :, :], ps[:, 0:FK * TT].rearrange("p (c t) -> p c t", c=FK),
                                                   ex_w[:, k:k + 1], None, ALU.mult), name)

                    def expert_out(tt):
                        ps = filled(dve, f"y{tt}")
                        read_out(dve.tensor_tensor(y[:, tt, :], hb[:, tt, :], ps[0:TT, 0:D], ALU.add), f"y{tt}")

                    walk({"norm": norm, "rows": rows, "batch_norm": batch_norm, "gelu_columns": gelu_columns,
                          "token_values": token_values, "route": route_, "gates": gates, "ffn": ffn, "stack": stack,
                          "v": v, "qk": qk_, "score": score, "max_split": max_split, "weigh": weigh,
                          "context": context, "mean": mean, "logits": logits, "mix_weights": mix_weights,
                          "bias_rows": bias_rows, "wo": wo_, "experts_chosen": experts_chosen,
                          "hidden_columns": hidden_columns, "expert_out": expert_out})

                @block.gpsimd
                def _(pool):
                    chain = [0]

                    def link(ins):
                        chain[0] += 1
                        ins.then_inc(pool_chain, 1)
                        pool.wait_ge(pool_chain, chain[0])

                    def norm(i):
                        _, _, eps, count = NORM[i]
                        _, mv, var, var_ready, rstd, rstd_ready, _ = BACK_NORM if i == 6 else FRONT_NORM
                        pool.wait_ge(var_ready, count)
                        link(pool.tensor_scalar(var[:, :], mv[:, :, 1], eps, None, ALU.add))
                        pool.tensor_tensor(rstd[:, :], var[:, :], neg_half[:, :], ALU.pow).then_inc(rstd_ready, 1)

                    def gelu(tt):
                        pool.wait_ge(ssq_ready, 2 * tt + 2)
                        link(pool.tensor_tensor(ssum[:, :], ssq[:, 0:1], ssq[:, 1:2], ALU.add))
                        link(pool.tensor_scalar(smean[:, :], ssum[:, :], 1.0 / NTOK, None, ALU.mult))
                        pool.tensor_tensor(a_scale[:, tt:tt + 1], smean[:, :], neg_half[:, 0:1], ALU.pow)\
                            .then_inc(a_scale_ready, 1)

                    def split(st, tt):
                        pool.wait_ge(hi_ready, 2 * (2 * POS[st] + tt + 1))
                        pool.tensor_tensor(q_stack[:, :, 2, :], qk[:, tt, 0, :, :], q_stack[:, :, 0, :].bitcast(F32),
                                           ALU.subtract).then_inc(lo_ready, 1)
                        pool.tensor_tensor(k_stack[:, :, 1, :], qk[:, tt, 1, :, :], k_stack[:, :, 0, :].bitcast(F32),
                                           ALU.subtract).then_inc(lo_ready, 1)

                    walk({"norm": norm, "gelu": gelu, "split": split})

            nc.all_engine_barrier(sems_to_clear=per_iteration)

        iteration(0, None, None)
        iteration(1, 0, None)
        with nc.Fori(0, B - 2) as clip:
            iteration(clip + 2, clip + 1, clip)
        iteration(None, B - 1, B - 2)
        with nc.Block() as block:
            @block.sync
            def _(sp):
                sp.dma_start(out[B - 1, :, :].rearrange("(t p) d -> p t d", p=TT), y).then_inc(y_stored, 16)
                sp.wait_ge(y_stored, 16)


def kernel(**inputs):
    import numpy as np
    import concourse.bacc as bacc
    from concourse.bass_utils import run_bass_kernel_spmd

    w = {name: np.asarray(a) for name, a in inputs.items()}

    def columns(a):
        return a.reshape(-1, 128, a.shape[-1]).transpose(1, 0, 2)

    mha = [[w[f"L1_ffn_mha_{n}"][m].reshape(D, H * HD) for n in ("wq", "wk", "wv")] for m in range(2)]
    qkv = [[w[f"L1_attn_{n}"].T for n in ("Wq", "Wk", "Wv")]] + mha
    arrays = {
        "x": w["x"],
        "conv_w": columns(w["L0_tok_W"].T),
        "conv_rows": np.stack([w["L0_tok_b"], w["L0_tok_gamma"], w["L0_tok_beta"],
                               w["L0_tok_running_mean"], w["L0_tok_running_var"]]),
        "keys": columns(w["L0_attn_key_param_tokens"].T),
        "values": columns(w["L0_attn_value_param_tokens"]),
        "route": columns(np.concatenate([w["L0_ffn_w_route"], w["L0_ffn_compress"]]).T),
        "routed": w["L0_ffn_routed"].transpose(0, 2, 1).reshape(E * R, D),
        "qkv_w": np.stack([columns(np.concatenate(s, axis=1)) for s in qkv], axis=1),
        "qkv_bias": np.stack([np.concatenate([w[f"L1_ffn_mha_{n}"][m].reshape(-1) for n in ("bq", "bk", "bv")])
                              for m in range(2)]),
        "wo": np.stack([columns(w["L1_ffn_mha_wo"][m].reshape(D, D)) for m in range(2)], axis=1),
        "bo": w["L1_ffn_mha_bo"],
        "ln_cols": np.stack([w[f"L1_ffn_{n}"].reshape(DK, 128).T for n in ("ln1_g", "ln1_b", "ln2_g", "ln2_b")], axis=1),
        "mix_rw": columns(w["L1_ffn_mha_rw"]),
        "mix_rb": w["L1_ffn_mha_rb"].reshape(1, -1),
        "ex_rw": columns(w["L1_ffn_ffn_rw"]),
        "ex_rb": w["L1_ffn_ffn_rb"].reshape(1, -1),
        "fw1": w["L1_ffn_fw1"].reshape(EX, DK, 128, F).transpose(2, 0, 1, 3).reshape(128, EX, DK * F),
        "fw2": w["L1_ffn_fw2"].reshape(EX, FK, 128, D).transpose(2, 0, 1, 3).reshape(128, EX, FK * D),
    }
    arrays = {name: np.ascontiguousarray(a) for name, a in arrays.items()}
    nc = bacc.Bacc("TRN2", target_bir_lowering=False, num_devices=1)
    inp = {name: nc.dram_tensor(f"in_{name}", shape, F32, kind="ExternalInput").ap() for name, shape in INPUTS.items()}
    out = nc.dram_tensor("out", [B, TP, D], F32, kind="ExternalOutput").ap()
    audio_tower(nc, inp, out)
    r = run_bass_kernel_spmd(nc, [{f"in_{name}": a for name, a in arrays.items()}], core_ids=[0])
    return r.results[0]["out"]
```

```python
from contextlib import ExitStack

import concourse.bass as bass
from concourse import mybir

F32 = mybir.dt.float32
F32R = mybir.dt.float32r
I32 = mybir.dt.int32
U32 = mybir.dt.uint32
ALU = mybir.AluOpType
ACT = mybir.ActivationFunctionType
AX = mybir.AxisListType

B, T, DIN = 32, 256, 128
CONTEXT = 5
TP = T - (CONTEXT - 1)
TT = TP // 2
D = 256
DK = D // 128
NTOK = 1024
NK = NTOK // 128
E, R = 8, 16
LORA_SCALE = 32.0 / R
H, HD = 16, 16
PAIRS = H // 2
SLOTS = 4
HW = SLOTS * HD
SETS = 3
SCALE = [1.0 / 16.0, 1.0 / 4.0, 1.0 / 4.0]
VW = 32
EX = 8
F = 2 * D
FK = F // 128
EPS = 1e-5
EPS_MIX = 1e-6
PT_RING = 8

INPUTS = {
    "x": [B, T, DIN], "conv_w": [128, CONTEXT, D], "conv_rows": [4, D], "bn_var": [128, DK],
    "keys": [128, DK, NTOK], "key_rows": [128, NK, D], "values": [128, NK, D], "route": [128, DK, E + R], "routed": [128, D],
    "qkv_w": [128, SETS, DK, 3 * D], "qk_bias": [2, 2 * D], "bv": [128, 2, DK], "wo": [128, 2, DK, D], "bo": [2, D],
    "ln_cols": [128, 4, DK], "mix_rw": [128, DK, 2], "mix_rb": [1, 2], "ex_rw": [128, DK, EX], "ex_rb": [1, EX],
    "fw1": [128, EX, DK * F], "fw2": [128, EX, FK * D],
}

ORDER = """
    x_columns_out hb score_out.1.0 score_out.1.1 score_out.1.2 score_out.1.3 score.1.0 score.1.1 score.1.2 score.1.3
    split.2.0 score_out.1.4 x_columns score_out.1.5 score.1.4 qk.2.0 qk_out.2.0 score.1.5 score_out.1.6 conv.0
    score_out.1.7 batch_norm stack_out.2.0 score_out.1.8 score_out.1.9 norm.1 score_out.1.10 score.1.6 score.1.7
    conv.1 stack.2.0 n1_out score.1.8 score.1.9 mean.0 score.1.10 rows.1 qk.2.1 score_out.1.11 score.1.11 qk_out.2.1
    score_out.1.12 score.1.12 gram_out split.2.1 score_out.1.13 mean_square_out n1 score_out.1.14 score.1.13
    diagonals stack_out.2.1 keys_out.0 keys_out.1 gram score.1.14 max_columns_out.1 mean_square keys_out.2
    keys_out.3 stack.2.1 spread logits.0 score.1.15 spread_out score.2.0 keys.0 keys.1 score_out.1.15 logits_exp.0
    max_split.1 score.2.1 attend_out.1.0 keys.2 attend_out.1.1 score.2.2 score_out.2.0 attend_out.1.2 score_out.2.1
    attend_out.1.3 score_out.2.2 attend_out.1.4 max_columns.1 keys.3 attend_out.1.5 attend_out.1.6 n2_out score.2.3
    attend_out.1.7 attend_out.1.8 token_values.0.0 score.2.4 attend.1.0 score_out.2.3 attend.1.1 token_values.0.1
    token_values.1.0 logits_out.0 mix_weights token_values_out.0.1 score_out.2.4 token_values_out.1.1 weigh_out.1.0
    token_values.1.1 attend.1.2 attend.1.3 attend.1.4 score.2.5 gap_exp attend_out.1.9 norm.2 rows.2 weigh.1.0
    attend_out.1.10 attend_out.1.11 score_out.2.5 attend.1.5 attend.1.6 score.2.6 n2 score_out.2.6 score_out.2.7
    route_out attend_out.1.12 attend.1.7 attend.1.8 score.2.7 gates route attend.1.9 attend.1.10 weigh.1.1
    attend.1.11 weigh_out.1.1 score_out.2.8 score.2.8 score_out.2.9 score_out.2.10 ffn_out attend.1.12 attend.1.13
    norm.3 ceg_columns score.2.9 score.2.10 ffn context_out.1.0 score.2.11 ceg_columns_out rows.3 score.2.12
    attend_out.1.13 attend_out.1.14 score_out.2.11 attend_out.1.15 score_out.2.12 score_out.2.13 weigh_out.1.2
    weigh_out.1.3 n3_out qk_out.0.0 context.1.0 split.0.0 max_columns_out.2 attend.1.14 attend.1.15 weigh.1.2
    score_out.2.14 weigh.1.3 score_out.2.15 n3 score.2.13 score.2.14 qk.0.0 context_out.1.1 score.2.15 context.1.1
    max_split.2 qk.0.1 v_out.2.0 qk_out.0.1 stack_out.0.0 bias_rows max_columns.2 v_out.2.1 v.2.0 split.0.1
    stack.0.0 attend_out.2.0 attend_out.2.1 v.2.1 cT_out.0 stack_out.0.1 attend.2.0 cT.0 wo_out.0 attend.2.1
    score_out.0.0 attend.2.2 attend.2.3 score_out.0.1 score_out.0.2 stack.0.1 attend_out.2.2 score_out.0.3
    attend_out.2.3 attend_out.2.4 score_out.0.4 wo.0 score_out.0.5 score_out.0.6 score.0.0 attend_out.2.5
    attend_out.2.6 attend_out.2.7 attend_out.2.8 attend_out.2.9 attend.2.4 attend_out.2.10 score.0.1 weigh.2.0
    weigh_out.2.0 score.0.2 attend.2.5 score.0.3 attend.2.6 weigh_out.2.1 score.0.4 attend.2.7 score.0.5
    score_out.0.7 score_out.0.8 attend.2.8 score_out.0.9 attend_out.2.11 score_out.0.10 attend_out.2.12 score.0.6
    score_out.0.11 attend.2.9 score_out.0.12 attend_out.2.13 score.0.7 attend_out.2.14 score_out.0.13 attend.2.10
    score.0.8 weigh.2.1 attend_out.2.15 score.0.9 score.0.10 weigh_out.2.2 attend.2.11 weigh_out.2.3 context.2.0
    score.0.11 context_out.2.0 attend.2.12 attend.2.13 score.0.12 score.0.13 score_out.0.14 max_columns_out.0
    attend.2.14 attend.2.15 score.0.14 score_out.0.15 max_split.0 score.0.15 cT_out.1 weigh.2.2 weigh.2.3
    max_columns.0 attend_out.0.0 attend_out.0.1 context_out.2.1 attend_out.0.2 attend_out.0.3 attend_out.0.4
    context.2.1 cT.1 attend_out.0.5 attend_out.0.6 attend_out.0.7 v_out.0.0 wo_out.1 v.0.0 wo.1 norm.6 attend.0.0
    attend.0.1 attend.0.2 attend.0.3 attend.0.4 rows.6 attend.0.5 v.0.1 attend.0.6 v_out.0.1 attend.0.7 n5_out
    attend_out.0.8 n5 weigh.0.0 mean.1 attend.0.8 attend.0.9 weigh_out.0.0 weigh_out.0.1 logits_out.1 weigh.0.1
    attend.0.10 attend_out.0.9 attend_out.0.10 attend_out.0.11 logits_exp.1 attend.0.11 experts_chosen
    context_out.0.0 attend_out.0.12 weigh_out.0.2 weigh_out.0.3 attend_out.0.13 attend_out.0.14
    hidden_columns_out.0.0 logits.1 context_out.0.1 attend_out.0.15 hidden_columns_out.0.1 norm.4 rows.4 context.0.0
    norm.5 rows.5 attend.0.12 attend.0.13 weigh.0.2 expert_sum_out.0 attend.0.14 attend.0.15 hidden.0.0 weigh.0.3
    hidden.0.1 hidden_columns.0.0 context.0.1 hidden_columns.0.1 hidden_out.0.0 hidden.1.0 expert_sum.0 qk_out.1.0
    qk_out.1.1 hidden.1.1 hidden_out.0.1 hidden_out.1.0 v_out.1.0 hidden_out.1.1 n4_out n4 hidden_columns.1.0
    split.1.0 hidden_columns_out.1.0 hidden_columns.1.1 qk.1.0 qk.1.1 v_out.1.1 stack_out.1.0 split.1.1 v.1.0 v.1.1
    stack.1.0 expert_sum.1 hidden_columns_out.1.1 expert_sum_out.1 stack_out.1.1 stack.1.1
"""
STAGES = [(name, *map(int, args)) for name, *args in (word.split(".") for word in ORDER.split())]
FRONT_STAGES = ("x_columns", "conv", "batch_norm", "n1", "gram", "mean_square", "diagonals", "spread", "keys",
                "token_values", "n2", "route", "gap_exp", "gates", "ceg_columns", "ffn", "n3", "n4")


def in_front(stage):
    name = stage[0].removesuffix("_out")
    if name in ("norm", "rows"):
        return stage[1] != 6
    if name in ("qk", "v", "split", "stack"):
        return stage[1] < 2
    shared = ("score", "attend", "max_split", "max_columns", "weigh", "context")
    return name in FRONT_STAGES or name in shared and stage[1] == 0


def fills(stage):
    name, args = stage[0], "".join(str(a) for a in stage[1:])
    if name == "stack":
        return [f"t{w}{args}{half}" for w in "qk" for half in range(2)]
    if name == "conv":
        return ["conv"] if args == "1" else []
    if name == "token_values":
        return [f"av{args[0]}"] if args[1] == "1" else []
    return {"n1": ["n1T"], "n2": ["n2T"], "n3": ["n3T"], "n4": ["n4T"], "n5": ["n5T"], "x_columns": ["xT"],
            "keys": ["a" + args], "gram": ["gn"], "mean_square": ["ms"], "spread": ["sp"], "route": ["rc"], "ceg_columns": ["cegT"],
            "ffn": ["ffn"], "qk": ["qk" + args], "v": ["v" + args], "max_columns": ["mx" + args],
            "weigh": ["o" + args], "context": ["c" + args], "cT": ["cT" + args], "wo": ["wo" + args],
            "logits": ["lg" + args], "hidden": ["h" + args], "hidden_columns": ["hT" + args],
            "expert_sum": ["y" + args]}.get(name, [])


FRONT_FILLS = [f for s in STAGES if in_front(s) for f in fills(s)]
BACK_FILLS = [f for s in STAGES if not in_front(s) for f in fills(s)]
TABLE = {1: 0, 2: 1, 0: 0}

LOADS = 13 + 10


def audio_tower(nc, inp, out):
    with ExitStack() as ctx:
        def sb(name, shape, dt=F32):
            return ctx.enter_context(nc.sbuf_tensor(name, shape, dt))

        def psum(name):
            return ctx.enter_context(nc.psum_tensor(name, [128, 512], F32))

        def sem(name):
            return ctx.enter_context(nc.semaphore(name))

        conv_w = sb("conv_w", [128, CONTEXT, D])
        conv_b = sb("conv_b", [TT, D])
        bn_a = sb("bn_a", [TT, D])
        bn_b = sb("bn_b", [TT, D])
        keys = sb("keys", [128, DK, NTOK])
        values = sb("values", [128, NK, D])
        route = sb("route", [128, DK, E + R])
        routed = sb("routed", [128, D])
        qkv_w = sb("qkv_w", [128, SETS, DK, 3 * D])
        qk_bias = sb("qk_bias", [TT, 2, 2 * D])
        wo = sb("wo", [128, 2, DK, D])
        bo = sb("bo", [TT, 2, D])
        ln_cols = sb("ln_cols", [128, 4, DK])
        mix_rw = sb("mix_rw", [128, DK, 2])
        mix_rb = sb("mix_rb", [128, 2])
        ex_rw = sb("ex_rw", [128, DK, EX])
        ex_rb = sb("ex_rb", [128, EX])
        fw1 = sb("fw1", [128, EX * DK * F])
        fw2 = sb("fw2", [128, EX * FK * D])
        identr = sb("identr", [128, 128], F32R)
        ident = identr[:, :].bitcast(F32)
        iota_i = sb("iota_i", [TT, E], I32)
        iota = sb("iota", [TT, E])
        neg_half = sb("neg_half", [128, 2])
        ones = sb("ones", [128, 1])
        bn_root = sb("bn_root", [128, DK])
        mean_sq = sb("mean_sq", [TT, 2])
        inv_root = sb("inv_root", [TT, 2])
        gram = sb("gram", [128, DK, D])
        bv = sb("bv", [128, 2, DK])

        gel_room = sb("gel_room", [128, NTOK])
        xs = gel_room[:, 0:2 * DIN].rearrange("p (t d) -> p t d", t=2)
        xT = gel_room[:, 2 * DIN:2 * DIN + T]
        nf = gel_room[0:TT, 2 * D:4 * D].rearrange("p (t d) -> p t d", t=2)
        ceg = gel_room[0:TT, 0:2 * E * R].rearrange("p (t e r) -> p t e r", t=2, e=E)
        gram_n = gel_room[:, 0:DK * TP].rearrange("p (k t) -> p k t", k=DK)
        diagonal = gel_room[0:TT, DK * TP:(DK + 1) * TP].rearrange("p (t f) -> p t f", t=2)
        cxT = gel_room[:, 0:2 * DK * TP].rearrange("p (m k t) -> p m k t", m=2, k=DK)
        hid = gel_room[0:TT, :].rearrange("p (e f) -> p e f", e=2)
        gel_low = sb("gel_low", [128, 4 * TP])
        gelT = [r.rearrange("p (k t) -> p k t", k=4) for r in (gel_low[:, :], gel_room[:, 0:4 * TP])]
        cegT = gel_low[:, 0:TP]
        hidT = gel_low[:, :].rearrange("p (e c t) -> p e c t", e=2, c=FK)
        hf = sb("hf", [TT, 2, D])
        nfT = sb("nfT", [128, DK, TP])
        f_stats = sb("f_stats", [TT, 2, 6])
        f_mv = sb("f_mv", [TT, 2, 2])
        f_var = sb("f_var", [TT, 2])
        f_rstd = sb("f_rstd", [TT, 2])
        rc = sb("rc", [TT, 2, E + R])
        top_v = sb("top_v", [TT, 2, 8])
        top_i = sb("top_i", [TT, 2, 8], U32)
        top_f = sb("top_f", [TT, 2, 8])
        gap = sb("gap", [TT, 2])
        gap_e = sb("gap_e", [TT, 2])
        gap_p = sb("gap_p", [TT, 2])
        w_first = sb("w_first", [TT, 2])
        w_second = sb("w_second", [TT, 2])
        gate = sb("gate", [TT, 2, E])
        gate2 = sb("gate2", [TT, 2, E])

        hb = sb("hb", [TT, 2, D])
        xm = sb("xm", [TT, 2, D])
        nb = sb("nb", [TT, 2, D])
        nbT = sb("nbT", [128, DK, TP])
        b_stats = sb("b_stats", [TT, 2, 6])
        b_mv = sb("b_mv", [TT, 2, 2])
        b_var = sb("b_var", [TT, 2])
        b_rstd = sb("b_rstd", [TT, 2])
        cx = nb[:, :, :]
        qk_room = sb("qk_room", [128, 2 * 2 * D])
        qk = qk_room[0:TT, :].rearrange("p (t w h d) -> p t w h d", t=2, w=2, h=H)
        vaug = sb("vaug", [TT, 2, H, VW])
        q_stack = sb("q_stack", [TT, H, SLOTS, HD], F32R)
        k_stack = sb("k_stack", [TT, H, SLOTS, HD], F32R)
        qT = [sb(f"qT{i}", [128, PAIRS, TP], F32R) for i in range(2)]
        kT = [sb(f"kT{i}", [128, PAIRS, TP], F32R) for i in range(2)]
        row_max = sb("row_max", [TT, 2, H])
        max_parts = sb("max_parts", [TT, 2, 2, 2, PAIRS], F32R)
        room = sb("room", [128, PT_RING * 2 * TP])
        probs = room[0:TT, :].rearrange("p (h k t) -> p h k t", h=PT_RING, k=2)
        maxT = room[0:32, (2 * PT_RING - 1) * TP:2 * PT_RING * TP]
        oT = sb("oT", [128, 2, TP])
        rec = sb("rec", [TT, 2, 8])
        msum = sb("msum", [128, DK])
        logit = sb("logit", [128, EX])
        neg_max = sb("neg_max", [128, 1])
        expo = sb("expo", [128, EX])
        esum = sb("esum", [128, 1])
        erec = sb("erec", [128, 1])
        mix_p = sb("mix_p", [128, 2])
        ex_p = sb("ex_p", [128, EX])
        ex_v = sb("ex_v", [128, 8])
        ex_i = sb("ex_i", [128, 8], U32)
        ex_o = sb("ex_o", [1, 8], I32)
        pair_sum = sb("pair_sum", [128, 1])
        pair_rec = sb("pair_rec", [128, 1])
        ex_w = sb("ex_w", [128, 2])
        y = hb[:, :, :]

        front_bank = [psum("front0"), psum("front1")]
        score_bank = [psum("score0"), psum("score1")]
        prob_bank = [psum("prob0"), psum("prob1")]
        back_bank = [psum("back0"), psum("back1")]

        loaded = sem("loaded")
        experts_loaded = sem("experts_loaded")
        const_ready = sem("const_ready")
        front_full = [sem("front_full0"), sem("front_full1")]
        front_read = [sem("front_read0"), sem("front_read1")]
        back_full = [sem("back_full0"), sem("back_full1")]
        back_read = [sem("back_read0"), sem("back_read1")]
        x_loaded = sem("x_loaded")
        f_var_ready = sem("f_var_ready")
        f_rstd_ready = sem("f_rstd_ready")
        f_n_ready = sem("f_n_ready")
        inv_root_ready = sem("inv_root_ready")
        diagonal_ready = sem("diagonal_ready")
        gap_ready = sem("gap_ready")
        gap_exp_ready = sem("gap_exp_ready")
        ceg_ready = sem("ceg_ready")
        hb_copied = sem("hb_copied")
        b_var_ready = sem("b_var_ready")
        b_rstd_ready = sem("b_rstd_ready")
        b_n_ready = sem("b_n_ready")
        hi_ready = sem("hi_ready")
        lo_ready = sem("lo_ready")
        scores_full = sem("scores_full")
        maxima_done = sem("maxima_done")
        parts_ready = sem("parts_ready")
        max_placed = sem("max_placed")
        shifted_full = sem("shifted_full")
        exp_done = sem("exp_done")
        msum_ready = sem("msum_ready")
        logit_ready = sem("logit_ready")
        softexp_ready = sem("softexp_ready")
        expert_ready = sem("expert_ready")
        y_stored = sem("y_stored")
        act_chain = sem("act_chain")
        dve_chain = sem("dve_chain")
        pool_chain = sem("pool_chain")
        per_iteration = range(front_full[0].num, pool_chain.num + 1)

        FILL = {}
        for fills, banks, full, read in ((FRONT_FILLS, front_bank, front_full, front_read),
                                         (BACK_FILLS, back_bank, back_full, back_read)):
            for n, name in enumerate(fills):
                FILL[name] = (banks[n % 2], full[n % 2], read[n % 2], n // 2 + 1)

        def filled(eng, name):
            ps, full, _, n = FILL[name]
            eng.wait_ge(full, n)
            return ps

        def wait_read(eng, name):
            _, _, read, n = FILL[name]
            eng.wait_ge(read, n)

        def read_out(ins, name):
            ins.then_inc(FILL[name][2], 1)

        eye = oT[:, 0, 0:128]
        key_rows = room[:, 0:NK * D].rearrange("p (k d) -> p k d", k=NK)
        bn_diagonal = room[:, NK * D:NK * D + D].rearrange("p (k d) -> p k d", k=DK)

        with nc.Block() as block:
            @block.sync
            def _(sp):
                for dst, name in ((conv_w, "conv_w"), (keys, "keys"), (values, "values"), (route, "route"),
                                  (routed, "routed"), (qkv_w, "qkv_w"), (wo, "wo"), (ln_cols, "ln_cols"),
                                  (mix_rw, "mix_rw"), (ex_rw, "ex_rw"), (bv, "bv"), (key_rows, "key_rows"),
                                  (bn_root, "bn_var")):
                    shape = INPUTS[name]
                    full = (slice(None),) * len(shape)
                    sp.dma_start(dst[full], inp[name][full]).then_inc(loaded, 16)
                rows = [(conv_b[:, :], inp["conv_rows"][0:1, :]),
                        (hf[:, 0, :], inp["conv_rows"][1:2, :]), (hf[:, 1, :], inp["conv_rows"][2:3, :]),
                        (nf[:, 0, :], inp["conv_rows"][3:4, :]),
                        (mix_rb[:, :], inp["mix_rb"][0:1, :]), (ex_rb[:, :], inp["ex_rb"][0:1, :])]
                rows += [(qk_bias[:, m, :], inp["qk_bias"][m:m + 1, :]) for m in range(2)]
                rows += [(bo[:, m, :], inp["bo"][m:m + 1, :]) for m in range(2)]
                for dst, src in rows:
                    sp.dma_start(dst, src[0, :].partition_broadcast(dst.shape[0])).then_inc(loaded, 16)
                sp.wait_ge(loaded, 16 * LOADS)

            @block.gpsimd
            def _(pool):
                pool.memset(eye, 0.0).then_inc(const_ready, 1)
                pool.wait_ge(const_ready, 1)
                pool.affine_select(out=eye, in_=eye, compare_op=ALU.not_equal, fill=1.0, base=0,
                                   pattern=[[-1, 128]], channel_multiplier=1).then_inc(const_ready, 1)
                pool.iota(iota_i[:, :], pattern=[[1, E]], base=0, channel_multiplier=0).then_inc(const_ready, 1)
                pool.memset(neg_half[:, :], -0.5).then_inc(const_ready, 1)
                pool.wait_ge(loaded, 16 * LOADS)
                pool.tensor_scalar(bn_root[:, :], bn_root[:, :], EPS, None, ALU.add).then_inc(pool_chain, 1)
                pool.wait_ge(pool_chain, 1)
                pool.wait_ge(const_ready, 4)
                pool.tensor_tensor(bn_root[:, :], bn_root[:, :], neg_half[:, :], ALU.pow).then_inc(f_rstd_ready, 1)

            @block.scalar
            def _(act):
                act.wait_ge(loaded, 16 * LOADS)
                for e in range(EX):
                    act.dma_start(fw1[:, e * DK * F:(e + 1) * DK * F], inp["fw1"][:, e, :]).then_inc(experts_loaded, 16)
                    act.dma_start(fw2[:, e * FK * D:(e + 1) * FK * D], inp["fw2"][:, e, :]).then_inc(experts_loaded, 16)

            @block.tensor
            def _(pe):
                pe.wait_ge(loaded, 16 * LOADS)
                for j in range(DK):
                    for k in range(NK):
                        last = pe.matmul(front_bank[0][:, j * D:(j + 1) * D], key_rows[:, k, j * 128:(j + 1) * 128],
                                         key_rows[:, k, :], start=k == 0, stop=k == NK - 1)
                last.then_inc(front_full[0], 1)
                for m in range(2):
                    for k in range(DK):
                        last = pe.matmul(front_bank[1][:, m * D:(m + 1) * D], bv[:, m, k:k + 1].broadcast_to([128, 128]),
                                         wo[:, m, k, :], start=k == 0, stop=k == DK - 1)
                last.then_inc(front_full[1], 1)
                pe.wait_ge(diagonal_ready, 1)
                for k in range(DK):
                    last = pe.matmul(back_bank[0][:, k * 128:(k + 1) * 128], ones[:, 0:1].broadcast_to([128, 128]),
                                     bn_diagonal[:, k, :], start=True, stop=True)
                last.then_inc(back_full[0], 1)

            @block.vector
            def _(dve):
                dve.wait_ge(const_ready, 3)
                dve.memset(ones[:, :], 1.0)
                dve.wait_ge(f_rstd_ready, 1)
                for k in range(DK):
                    last = dve.tensor_scalar(bn_diagonal[:, k, :], eye, bn_root[:, k:k + 1], None, ALU.mult)
                last.then_inc(diagonal_ready, 1)
                dve.wait_ge(loaded, 16 * LOADS)
                dve.wait_ge(front_full[0], 1)
                dve.tensor_copy(gram[:, :, :], front_bank[0][:, :].rearrange("p (j d) -> p j d", j=DK))
                dve.wait_ge(front_full[1], 1)
                dve.tensor_tensor(bo[:, :, :], bo[:, :, :], front_bank[1][0:TT, :].rearrange("p (m d) -> p m d", m=2),
                                  ALU.add)
                dve.wait_ge(back_full[0], 1)
                dve.tensor_tensor(bn_a[:, :], back_bank[0][0:TT, 0:D], hf[:, 0, :], ALU.mult).then_inc(dve_chain, 1)
                dve.wait_ge(dve_chain, 1)
                dve.tensor_tensor(nf[:, 0, :], nf[:, 0, :], bn_a[:, :], ALU.mult).then_inc(dve_chain, 1)
                dve.wait_ge(dve_chain, 2)
                dve.tensor_tensor(bn_b[:, :], hf[:, 1, :], nf[:, 0, :], ALU.subtract)
                dve.tensor_copy(identr[:, :], eye)
                dve.tensor_copy(iota[:, :], iota_i[:, :])
                dve.memset(q_stack[:, :, 3, :].bitcast(F32), 0.0)
                dve.memset(k_stack[:, :, 3, 2:HD].bitcast(F32), 0.0)
                dve.memset(k_stack[:, :, 3, 0:2].bitcast(F32), -1.0)
                dve.memset(vaug[:, :, :, HD:VW], 1.0)

        nc.all_engine_barrier(sems_to_clear=per_iteration)

        def iteration(front, back, stored):
            F_ON, B_ON = front is not None, back is not None
            SEQ = [1] * B_ON + [2] * B_ON + [0] * F_ON
            POS = {st: n for n, st in enumerate(SEQ)}
            STACKED = [2] * B_ON + [0, 1] * F_ON
            STACK_POS = {st: n for n, st in enumerate(STACKED)}

            def before(st, seq=SEQ):
                return seq[seq.index(st) - 1] if seq.index(st) else None

            def walk(parts):
                for stage in STAGES:
                    if (F_ON if in_front(stage) else B_ON) and stage[0] in parts:
                        parts[stage[0]](*stage[1:])

            NORM = {1: (hf, nf, EPS, 1), 2: (hf, nf, EPS, 2), 3: (hf, nf, EPS, 3), 4: (hf, xm, EPS, 4),
                    5: (xm, nb, EPS_MIX, 5), 6: (xm, nb, EPS_MIX, 1)}
            FRONT_NORM = (f_stats, f_mv, f_var, f_var_ready, f_rstd, f_rstd_ready, f_n_ready)
            BACK_NORM = (b_stats, b_mv, b_var, b_var_ready, b_rstd, b_rstd_ready, b_n_ready)

            with nc.Block(no_gpsimd_drain=True) as block:
                @block.sync
                def _(sp):
                    if F_ON:
                        sp.dma_start(xs, inp["x"][front, :, :].rearrange("(t p) d -> p t d", p=128))\
                          .then_inc(x_loaded, 16)
                    if stored is not None:
                        sp.dma_start(out[stored, :, :].rearrange("(t p) d -> p t d", p=TT), y)\
                          .then_inc(y_stored, 16)
                    for st in SEQ:
                        wait_read(sp, f"mx{st}")
                        for j in range(2):
                            row = HW * j + 3 * HD
                            sp.dma_start(qT[TABLE[st]][row:row + 2, :, :].bitcast(F32),
                                         maxT[2 * PAIRS * j:2 * PAIRS * (j + 1), :]).then_inc(max_placed, 16)
                    if not B_ON:
                        sp.wait_ge(experts_loaded, 16 * 2 * EX)
                    if F_ON:
                        sp.wait_ge(x_loaded, 16)
                    if stored is not None:
                        sp.wait_ge(y_stored, 16)

                @block.tensor
                def _(pe):
                    chosen = []

                    def take(name):
                        ps, _, read, n = FILL[name]
                        if n > 1:
                            pe.wait_ge(read, n - 1)
                        return ps

                    def done(name, ins):
                        ins.then_inc(FILL[name][1], 1)

                    def turn(name, src):
                        ps = take(name)
                        for tt in range(2):
                            for k in range(DK):
                                c = k * TP + tt * TT
                                last = pe.transpose(ps[:, c:c + TT], src[:, tt, k * 128:(k + 1) * 128],
                                                    ident[0:TT, 0:TT])
                        done(name, last)

                    def x_columns():
                        pe.wait_ge(x_loaded, 16)
                        ps = take("xT")
                        for t in range(2):
                            last = pe.transpose(ps[:, t * 128:(t + 1) * 128], xs[:, t, :], ident)
                        done("xT", last)

                    def conv(tt):
                        ps = FILL["conv"][0]
                        if tt == 0:
                            take("conv")
                            wait_read(pe, "xT")
                        for c in range(CONTEXT):
                            last = pe.matmul(ps[0:TT, tt * D:(tt + 1) * D], xT[:, tt * TT + c:tt * TT + c + TT],
                                             conv_w[:, c, :], start=c == 0, stop=c == CONTEXT - 1)
                        if tt:
                            done("conv", last)

                    def n1():
                        pe.wait_ge(f_n_ready, 1)
                        turn("n1T", nf)

                    def n2():
                        pe.wait_ge(f_n_ready, 2)
                        turn("n2T", nf)

                    def n3():
                        pe.wait_ge(f_n_ready, 3)
                        turn("n3T", nf)

                    def n4():
                        pe.wait_ge(f_n_ready, 5)
                        turn("n4T", nb)

                    def n5():
                        pe.wait_ge(b_n_ready, 1)
                        turn("n5T", nb)

                    def gram_():
                        wait_read(pe, "n1T")
                        ps = take("gn")
                        for j in range(DK):
                            for k in range(DK):
                                last = pe.matmul(ps[:, j * TP:(j + 1) * TP], gram[:, k, j * 128:(j + 1) * 128],
                                                 nfT[:, k, :], start=k == 0, stop=k == DK - 1)
                        done("gn", last)

                    def mean_square():
                        wait_read(pe, "gn")
                        ps = take("ms")
                        for tt in range(2):
                            for k in range(DK):
                                last = pe.matmul(ps[0:TT, tt:tt + 1], gram_n[:, k, tt * TT:(tt + 1) * TT], ones[:, 0:1],
                                                 start=k == 0, stop=k == DK - 1)
                        done("ms", last)

                    def spread():
                        pe.wait_ge(diagonal_ready, 1)
                        ps = take("sp")
                        for tt in range(2):
                            last = pe.matmul(ps[:, tt * TT:(tt + 1) * TT], ones[0:TT, 0:1].broadcast_to([TT, 128]),
                                             diagonal[:, tt, :], start=True, stop=True)
                        done("sp", last)

                    def keys_(pair):
                        if pair == 0:
                            wait_read(pe, "sp")
                        name = f"a{pair}"
                        ps = take(name)
                        for c in range(2):
                            blk = 2 * pair + c
                            for k in range(DK):
                                last = pe.matmul(ps[:, c * TP:(c + 1) * TP], keys[:, k, blk * 128:(blk + 1) * 128],
                                                 nfT[:, k, :], start=k == 0, stop=k == DK - 1)
                        done(name, last)

                    def token_values(tt, half):
                        name = f"av{tt}"
                        ps = take(name) if half == 0 else FILL[name][0]
                        if tt == 0:
                            wait_read(pe, f"a{2 * half}")
                            wait_read(pe, f"a{2 * half + 1}")
                        for blk in range(4 * half, 4 * half + 4):
                            last = pe.matmul(ps[0:TT, 0:D], gelT[half][:, blk % 4, tt * TT:(tt + 1) * TT],
                                             values[:, blk, :], start=blk == 0, stop=blk == NK - 1)
                        if half:
                            done(name, last)

                    def route_():
                        ps = take("rc")
                        wait_read(pe, "n2T")
                        for tt in range(2):
                            for k in range(DK):
                                last = pe.matmul(ps[0:TT, tt * 32:tt * 32 + E + R], nfT[:, k, tt * TT:(tt + 1) * TT],
                                                 route[:, k, :], start=k == 0, stop=k == DK - 1)
                        done("rc", last)

                    def ceg_columns():
                        pe.wait_ge(ceg_ready, 1)
                        ps = take("cegT")
                        for tt in range(2):
                            last = pe.transpose(ps[:, tt * TT:(tt + 1) * TT],
                                                ceg[:, tt, :, :].rearrange("p e r -> p (e r)"), ident[0:TT, 0:TT])
                        done("cegT", last)

                    def ffn():
                        ps = take("ffn")
                        wait_read(pe, "cegT")
                        for tt in range(2):
                            last = pe.matmul(ps[0:TT, tt * D:(tt + 1) * D], cegT[:, tt * TT:(tt + 1) * TT],
                                             routed[:, :], start=True, stop=True)
                        done("ffn", last)

                    def project(what, st, tt, lo, hi):
                        src = nbT if st else nfT
                        ps = take(f"{what}{st}{tt}")
                        for k in range(DK):
                            last = pe.matmul(ps[0:TT, 0:hi - lo], src[:, k, tt * TT:(tt + 1) * TT],
                                             qkv_w[:, st, k, lo:hi], start=k == 0, stop=k == DK - 1)
                        done(f"{what}{st}{tt}", last)

                    def qk_(st, tt):
                        if st < 2:
                            wait_read(pe, ("n3T", "n4T")[st])
                        project("qk", st, tt, 0, 2 * D)

                    def v(st, tt):
                        project("v", st, tt, 2 * D, 3 * D)

                    def stack(st, tt):
                        n = 2 * (2 * STACK_POS[st] + tt + 1)
                        pe.wait_ge(hi_ready, n)
                        pe.wait_ge(lo_ready, n)
                        for w, src in (("q", q_stack), ("k", k_stack)):
                            for half in range(2):
                                name = f"t{w}{st}{tt}{half}"
                                ps = take(name)
                                for c in range(4):
                                    p = 4 * half + c
                                    last = pe.transpose(ps[:, c * TT:(c + 1) * TT].bitcast(F32R),
                                                        src[:, 2 * p:2 * p + 2, :, :].rearrange("q h s d -> q (h s d)"),
                                                        identr[0:TT, 0:TT])
                                done(name, last)

                    def score(st, h):
                        n = H * POS[st] + h
                        if h == 0 and st != 1:
                            for tt in range(2):
                                for w in "qk":
                                    for half in range(2):
                                        wait_read(pe, f"t{w}{st}{tt}{half}")
                        if n >= 2:
                            pe.wait_ge(maxima_done, n - 1)
                        p, r = h // 2, HW * (h % 2)
                        for tt in range(2):
                            last = pe.matmul(score_bank[n % 2][0:TT, tt * TP:(tt + 1) * TP],
                                             qT[TABLE[st]][r:r + HW, p, tt * TT:(tt + 1) * TT],
                                             kT[TABLE[st]][r:r + HW, p, :], start=True, stop=True)
                        last.then_inc(scores_full, 1)

                    def max_columns(st):
                        pe.wait_ge(parts_ready, POS[st] + 1)
                        ps = take(f"mx{st}")
                        for tt in range(2):
                            last = pe.transpose(ps[0:32, tt * TT:(tt + 1) * TT].bitcast(F32R),
                                                max_parts[:, tt, :, :, :].rearrange("q j s p -> q (j s p)"),
                                                identr[0:TT, 0:TT])
                        done(f"mx{st}", last)

                    def attend(st, h):
                        n = H * POS[st] + h
                        if h == 0:
                            pe.wait_ge(max_placed, 32 * (POS[st] + 1))
                        if n >= 2:
                            pe.wait_ge(exp_done, n - 1)
                        p, r = h // 2, HW * (h % 2)
                        for tt in range(2):
                            last = pe.matmul(prob_bank[n % 2][0:TT, tt * TP:(tt + 1) * TP],
                                             kT[TABLE[st]][r:r + HW, p, tt * TT:(tt + 1) * TT],
                                             qT[TABLE[st]][r:r + HW, p, :], start=True, stop=True)
                        last.then_inc(shifted_full, 1)

                    def weigh(st, g):
                        pe.wait_ge(exp_done, H * POS[st] + 4 * g + 4)
                        if g == 0 and st != 1:
                            wait_read(pe, f"v{st}0")
                            wait_read(pe, f"v{st}1")
                        ps = take(f"o{st}{g}")
                        for tt in range(2):
                            for c in range(4):
                                h = 4 * g + c
                                last = pe.matmul(ps[32 * c:32 * c + 32, 0:TP], vaug[:, tt, h, :],
                                                 probs[:, h % PT_RING, tt, :], start=tt == 0, stop=tt == 1,
                                                 skip_group_check=True)
                        done(f"o{st}{g}", last)

                    def context(st, gg):
                        wait_read(pe, f"o{st}{2 * gg}")
                        wait_read(pe, f"o{st}{2 * gg + 1}")
                        ps = take(f"c{st}{gg}")
                        for g in range(2):
                            for tt in range(2):
                                c = (2 * tt + g) * 128
                                last = pe.transpose(ps[0:TT, c:c + 128], oT[:, g, tt * TT:(tt + 1) * TT], ident)
                        done(f"c{st}{gg}", last)

                    def logits(i):
                        w, n = ((mix_rw, 2), (ex_rw, EX))[i]
                        pe.wait_ge(msum_ready, i + 1)
                        ps = take(f"lg{i}")
                        for k in range(DK):
                            last = pe.matmul(ps[:, 0:n], msum[:, k:k + 1].broadcast_to([128, 128]), w[:, k, :],
                                             start=k == 0, stop=k == DK - 1)
                        done(f"lg{i}", last)

                    def cT(m):
                        wait_read(pe, f"c{m + 1}0")
                        wait_read(pe, f"c{m + 1}1")
                        turn(f"cT{m}", cx)

                    def wo_(m):
                        ps = take(f"wo{m}")
                        wait_read(pe, f"cT{m}")
                        for tt in range(2):
                            for k in range(DK):
                                last = pe.matmul(ps[0:TT, tt * D:(tt + 1) * D], cxT[:, m, k, tt * TT:(tt + 1) * TT],
                                                 wo[:, m, k, :], start=k == 0, stop=k == DK - 1)
                        done(f"wo{m}", last)

                    def hidden(tt, k):
                        if (tt, k) == (0, 0):
                            pe.wait_ge(expert_ready, 1)
                            chosen.extend(pe.value_load(ex_o[0:1, i:i + 1], min_val=0, max_val=EX - 1)
                                          for i in range(2))
                        ps = take(f"h{tt}{k}")
                        for d in range(DK):
                            last = pe.matmul(ps[0:TT, :], nbT[:, d, tt * TT:(tt + 1) * TT],
                                             fw1[:, bass.ds(chosen[k] * (DK * F) + d * F, F)],
                                             start=d == 0, stop=d == DK - 1)
                        done(f"h{tt}{k}", last)

                    def hidden_columns(tt, k):
                        wait_read(pe, f"h{tt}{k}")
                        ps = take(f"hT{tt}{k}")
                        for c in range(FK):
                            last = pe.transpose(ps[:, c * TT:(c + 1) * TT], hid[:, k, c * 128:(c + 1) * 128],
                                                ident[0:TT, 0:TT])
                        done(f"hT{tt}{k}", last)

                    def expert_sum(tt):
                        ps = take(f"y{tt}")
                        for k in range(2):
                            wait_read(pe, f"hT{tt}{k}")
                            for c in range(FK):
                                last = pe.matmul(ps[0:TT, 0:D], hidT[:, k, c, :],
                                                 fw2[:, bass.ds(chosen[k] * (FK * D) + c * D, D)],
                                                 start=k + c == 0, stop=k + c == FK)
                        done(f"y{tt}", last)

                    walk({"x_columns": x_columns, "conv": conv, "n1": n1, "n2": n2, "n3": n3, "n4": n4, "n5": n5,
                          "gram": gram_, "mean_square": mean_square, "spread": spread, "keys": keys_, "token_values": token_values,
                          "route": route_,
                          "ceg_columns": ceg_columns, "ffn": ffn, "qk": qk_, "v": v, "stack": stack, "score": score,
                          "max_columns": max_columns, "attend": attend, "weigh": weigh, "context": context,
                          "logits": logits, "cT": cT, "wo": wo_, "hidden": hidden, "hidden_columns": hidden_columns,
                          "expert_sum": expert_sum})

                @block.scalar
                def _(act):
                    def columns(name, dst):
                        ps = filled(act, name)
                        read_out(act.copy(dst, ps[:, 0:DK * TP].rearrange("p (k t) -> p k t", k=DK)), name)

                    def gained_columns(name, i):
                        ps = filled(act, name)
                        for k in range(DK):
                            last = act.activation(nbT[:, k, :], ps[:, k * TP:(k + 1) * TP], ACT.Identity,
                                                  scale=ln_cols[:, i, k:k + 1], bias=ln_cols[:, i + 1, k:k + 1])
                        read_out(last, name)

                    def x_columns():
                        ps = filled(act, "xT")
                        read_out(act.copy(xT, ps[:, 0:T]), "xT")

                    def n1():
                        columns("n1T", nfT[:, :, :])

                    def n2():
                        columns("n2T", nfT[:, :, :])

                    def n3():
                        columns("n3T", nfT[:, :, :])

                    def n4():
                        if B_ON:
                            filled(act, "h11")
                        gained_columns("n4T", 0)

                    def n5():
                        gained_columns("n5T", 2)

                    def hb_():
                        if stored is not None:
                            act.wait_ge(y_stored, 16)
                        act.copy(hb[:, :, :], hf[:, :, :]).then_inc(hb_copied, 1)

                    def keys_(pair):
                        name = f"a{pair}"
                        ps = filled(act, name)
                        blk = 2 * (pair % 2)
                        read_out(act.activation(gelT[pair // 2][:, blk:blk + 2, :],
                                                ps[:, 0:2 * TP].rearrange("p (c t) -> p c t", c=2), ACT.Gelu), name)

                    def gap_exp():
                        act.wait_ge(gap_ready, 1)
                        act.activation(gap_e[:, :], gap[:, :], ACT.Exp).then_inc(gap_exp_ready, 1)

                    def ceg_columns():
                        ps = filled(act, "cegT")
                        read_out(act.copy(cegT[:, :], ps[:, 0:TP]), "cegT")

                    def qk_(st, tt):
                        if st == 0:
                            ps = filled(act, f"qk0{tt}")
                            if STACK_POS[0]:
                                act.wait_ge(lo_ready, 2 * (2 * (STACK_POS[0] - 1) + tt + 1))
                            read_out(act.copy(qk[:, tt, :, :, :].rearrange("p w h d -> p (w h d)"), ps[0:TT, :]),
                                     f"qk0{tt}")

                    def split(st, tt):
                        wait_read(act, f"qk{st}{tt}")
                        last = (st, 0) if tt else (before(st, STACKED), 1)
                        if last[0] is not None:
                            filled(act, f"tq{last[0]}{last[1]}1")
                            filled(act, f"tk{last[0]}{last[1]}1")
                        act.copy(q_stack[:, :, 0:2, :],
                                 qk[:, tt, 0, :, :].unsqueeze(2).broadcast_to([TT, H, 2, HD])).then_inc(hi_ready, 1)
                        act.copy(k_stack[:, :, 0:3:2, :],
                                 qk[:, tt, 1, :, :].unsqueeze(2).broadcast_to([TT, H, 2, HD])).then_inc(hi_ready, 1)

                    def stack(st, tt):
                        if (st, tt) == (0, 0) and B_ON:
                            act.wait_ge(exp_done, H)
                        if (st, tt) == (1, 0):
                            act.wait_ge(exp_done, H * (POS[0] + 1))
                        for half in range(2):
                            name = f"tq{st}{tt}{half}"
                            ps = filled(act, name)
                            read_out(act.copy(qT[TABLE[st]][:, 4 * half:4 * half + 4, tt * TT:(tt + 1) * TT],
                                              ps[:, 0:4 * TT].rearrange("p (c t) -> p c t", c=4)), name)

                    def max_columns(st):
                        ps = filled(act, f"mx{st}")
                        if before(st) is not None:
                            act.wait_ge(max_placed, 32 * POS[st])
                            filled(act, f"o{before(st)}3")
                        read_out(act.copy(maxT, ps[0:32, 0:TP]), f"mx{st}")

                    def attend(st, h):
                        n = H * POS[st] + h
                        act.wait_ge(shifted_full, n + 1)
                        if n % 4 == 0 and n >= PT_RING:
                            g = n // 4 - 2
                            filled(act, f"o{SEQ[g // 4]}{g % 4}")
                        act.activation(probs[:, h % PT_RING, :, :],
                                       prob_bank[n % 2][0:TT, 0:2 * TP].rearrange("p (k t) -> p k t", k=2),
                                       ACT.Exp, scale=SCALE[st]).then_inc(exp_done, 1)

                    def weigh(st, g):
                        if st == 0:
                            return
                        ps = filled(act, f"o{st}{g}")
                        if g >= 2:
                            filled(act, f"c{st}0")
                        elif before(st) is not None:
                            filled(act, f"c{before(st)}1")
                        read_out(act.copy(oT[:, g % 2, :], ps[:, 0:TP]), f"o{st}{g}")

                    def logits_exp(i):
                        n = (2, EX)[i]
                        act.wait_ge(logit_ready, i + 1)
                        act.activation(expo[:, 0:n], logit[:, 0:n], ACT.Exp, bias=neg_max[:, :],
                                       accum_out=esum[:, :]).then_inc(softexp_ready, 1)

                    def cT(m):
                        columns(f"cT{m}", cxT[:, m, :, :])

                    def hidden(tt, k):
                        ps = filled(act, f"h{tt}{k}")
                        if tt:
                            filled(act, f"hT0{k}")
                        read_out(act.activation(hid[:, k, :], ps[0:TT, :], ACT.Gelu), f"h{tt}{k}")

                    walk({"x_columns_out": x_columns, "n1_out": n1, "n2_out": n2, "n3_out": n3, "n4_out": n4,
                          "n5_out": n5, "hb": hb_, "keys_out": keys_, "gap_exp": gap_exp,
                          "ceg_columns_out": ceg_columns, "qk_out": qk_, "split": split, "stack_out": stack,
                          "max_columns_out": max_columns, "attend_out": attend, "weigh_out": weigh,
                          "logits_exp": logits_exp, "cT_out": cT, "hidden_out": hidden})

                @block.vector
                def _(dve):
                    chain = [0]

                    def link(ins):
                        chain[0] += 1
                        ins.then_inc(dve_chain, 1)
                        dve.wait_ge(dve_chain, chain[0])

                    def norm(i):
                        h = NORM[i][0]
                        stats, mv, _, var_ready, _, _, _ = BACK_NORM if i == 6 else FRONT_NORM
                        if i == 3:
                            wait_read(dve, "ffn")
                        if i == 4:
                            wait_read(dve, "c00")
                            wait_read(dve, "c01")
                            link(dve.tensor_tensor(hf[:, :, :], hf[:, :, :], cx[:, :, :], ALU.add))
                        if i == 5:
                            dve.wait_ge(f_n_ready, 4)
                        if i == 6:
                            wait_read(dve, "wo1")
                        for tt in range(2):
                            last = dve.bn_stats(stats[:, tt, :], h[:, tt, :])
                        link(last)
                        for tt in range(2):
                            last = dve.bn_aggr(mv[:, tt, :], stats[:, tt, :])
                        last.then_inc(var_ready, 1)
                        if i == 6:
                            dve.wait_ge(hb_copied, 1)
                            link(dve.tensor_tensor(hb[:, :, :], hb[:, :, :], xm[:, :, :], ALU.add))

                    def rows(i):
                        h, n, _, count = NORM[i]
                        _, mv, _, var_ready, rstd, rstd_ready, n_ready = BACK_NORM if i == 6 else FRONT_NORM
                        dve.wait_ge(var_ready, count)
                        dve.wait_ge(rstd_ready, count)
                        for tt in range(2):
                            last = dve.tensor_scalar(n[:, tt, :], h[:, tt, :], mv[:, tt, 0:1], rstd[:, tt:tt + 1],
                                                     ALU.subtract, ALU.mult)
                        last.then_inc(n_ready, 1)

                    def both(row):
                        return row.unsqueeze(1).broadcast_to([TT, 2, D])

                    def batch_norm():
                        ps = filled(dve, "conv")
                        if B_ON:
                            dve.wait_ge(hb_copied, 1)
                        read_out(dve.tensor_tensor(hf[:, :, :], ps[0:TT, :].rearrange("p (t d) -> p t d", t=2),
                                                   both(conv_b[:, :]), ALU.add), "conv")
                        wait_read(dve, "conv")
                        link(dve.scalar_tensor_tensor(hf[:, :, :], hf[:, :, :], 0.0, both(bn_a[:, :]),
                                                      ALU.max, ALU.mult))
                        link(dve.tensor_tensor(hf[:, :, :], hf[:, :, :], both(bn_b[:, :]), ALU.add))

                    def gram_():
                        ps = filled(dve, "gn")
                        read_out(dve.tensor_tensor(gram_n, ps[:, 0:DK * TP].rearrange("p (k t) -> p k t", k=DK),
                                                   nfT[:, :, :], ALU.mult), "gn")

                    def mean_square():
                        ps = filled(dve, "ms")
                        read_out(dve.tensor_scalar(mean_sq[:, :], ps[0:TT, 0:2], 1.0 / NTOK, None, ALU.mult), "ms")

                    def diagonals():
                        dve.wait_ge(inv_root_ready, 1)
                        for tt in range(2):
                            last = dve.tensor_scalar(diagonal[:, tt, :], ident[0:TT, 0:TT], inv_root[:, tt:tt + 1], None,
                                                     ALU.mult)
                        last.then_inc(diagonal_ready, 1)

                    def spread():
                        ps = filled(dve, "sp")
                        read_out(dve.tensor_tensor(nfT[:, :, :], nfT[:, :, :],
                                                   ps[:, 0:TP].unsqueeze(1).broadcast_to([128, DK, TP]), ALU.mult), "sp")

                    def token_values(tt, half):
                        if half:
                            ps = filled(dve, f"av{tt}")
                            read_out(dve.tensor_tensor(hf[:, tt, :], hf[:, tt, :], ps[0:TT, 0:D], ALU.add), f"av{tt}")
                            if tt:
                                wait_read(dve, "av0")
                                wait_read(dve, "av1")

                    def route_():
                        ps = filled(dve, "rc")
                        read_out(dve.tensor_copy(rc[:, :, :], ps[0:TT, 0:64].rearrange("p (t c) -> p t c", t=2)
                                                 [:, :, 0:E + R]), "rc")
                        wait_read(dve, "rc")
                        for tt in range(2):
                            last = dve.max(top_v[:, tt, :], rc[:, tt, 0:E])
                        link(last)
                        dve.tensor_tensor(gap[:, :], top_v[:, :, 1], top_v[:, :, 0], ALU.subtract)\
                           .then_inc(gap_ready, 1)
                        for tt in range(2):
                            last = dve.max_index(top_i[:, tt, :], top_v[:, tt, :], rc[:, tt, 0:E])
                        link(last)
                        link(dve.tensor_copy(top_f[:, :, :], top_i[:, :, :]))

                    def gates():
                        dve.wait_ge(gap_exp_ready, 1)
                        link(dve.tensor_scalar(gap_p[:, :], gap_e[:, :], 1.0, None, ALU.add))
                        link(dve.reciprocal(w_first[:, :], gap_p[:, :]))
                        link(dve.tensor_tensor(w_second[:, :], gap_e[:, :], w_first[:, :], ALU.mult))
                        for tt in range(2):
                            dve.tensor_scalar(gate[:, tt, :], iota[:, :], top_f[:, tt, 0:1], w_first[:, tt:tt + 1],
                                              ALU.is_equal, ALU.mult)
                            last = dve.tensor_scalar(gate2[:, tt, :], iota[:, :], top_f[:, tt, 1:2],
                                                     w_second[:, tt:tt + 1], ALU.is_equal, ALU.mult)
                        link(last)
                        link(dve.tensor_tensor(gate[:, :, :], gate[:, :, :], gate2[:, :, :], ALU.add))
                        dve.tensor_tensor(ceg[:, :, :, :], gate[:, :, :].unsqueeze(3).broadcast_to([TT, 2, E, R]),
                                          rc[:, :, E:E + R].unsqueeze(2).broadcast_to([TT, 2, E, R]),
                                          ALU.mult).then_inc(ceg_ready, 1)

                    def ffn():
                        ps = filled(dve, "ffn")
                        read_out(dve.scalar_tensor_tensor(hf[:, :, :], ps[0:TT, :].rearrange("p (t d) -> p t d", t=2),
                                                          LORA_SCALE, hf[:, :, :], ALU.mult, ALU.add), "ffn")

                    def stack(st, tt):
                        if (st, tt) == (0, 0) and B_ON:
                            dve.wait_ge(exp_done, H)
                        if (st, tt) == (1, 0):
                            dve.wait_ge(exp_done, H * (POS[0] + 1))
                        for half in range(2):
                            name = f"tk{st}{tt}{half}"
                            ps = filled(dve, name)
                            read_out(dve.tensor_copy(kT[TABLE[st]][:, 4 * half:4 * half + 4, tt * TT:(tt + 1) * TT],
                                                     ps[:, 0:4 * TT].rearrange("p (c t) -> p c t", c=4)), name)

                    def v(st, tt):
                        name = f"v{st}{tt}"
                        ps = filled(dve, name)
                        last = 0 if st == 1 else before(st)
                        if last is not None:
                            filled(dve, f"o{last}3")
                        src = ps[0:TT, 0:D].rearrange("p (h d) -> p h d", h=H)
                        dst = vaug[:, tt, :, 0:HD]
                        read_out(dve.tensor_copy(dst, src), name)

                    def qk_(st, tt):
                        if st:
                            name = f"qk{st}{tt}"
                            ps = filled(dve, name)
                            if before(st, STACKED) is not None:
                                dve.wait_ge(lo_ready, 2 * (2 * (STACK_POS[st] - 1) + tt + 1))
                            read_out(dve.tensor_tensor(qk[:, tt, :, :, :].rearrange("p w h d -> p (w h d)"), ps[0:TT, :],
                                                       qk_bias[:, st - 1, 0:2 * D], ALU.add), name)

                    def score(st, h):
                        n = H * POS[st] + h
                        if h == 0 and before(st) is not None:
                            dve.wait_ge(parts_ready, POS[st])
                        dve.wait_ge(scores_full, n + 1)
                        dve.tensor_reduce(row_max[:, :, h], score_bank[n % 2][0:TT, 0:2 * TP]
                                          .rearrange("p (t k) -> p t k", t=2), AX.X, ALU.max).then_inc(maxima_done, 1)

                    def max_split(st):
                        dve.wait_ge(maxima_done, H * (POS[st] + 1))
                        if before(st) is not None:
                            filled(dve, f"mx{before(st)}")
                        src = row_max[:, :, :].rearrange("q t (p j) -> q t j p", j=2)
                        link(dve.tensor_copy(max_parts[:, :, :, 0, :], src))
                        dve.tensor_tensor(max_parts[:, :, :, 1, :], src, max_parts[:, :, :, 0, :].bitcast(F32),
                                          ALU.subtract).then_inc(parts_ready, 1)

                    def weigh(st, g):
                        if st:
                            return
                        ps = filled(dve, f"o{st}{g}")
                        if g >= 2:
                            filled(dve, f"c{st}0")
                        elif before(st) is not None:
                            filled(dve, f"c{before(st)}1")
                        read_out(dve.tensor_copy(oT[:, g % 2, :], ps[:, 0:TP]), f"o{st}{g}")

                    def context(st, gg):
                        name = f"c{st}{gg}"
                        ps = filled(dve, name)
                        src = ps[0:TT, :].rearrange("p (t h w) -> p t h w", t=2, w=VW)
                        link(dve.reciprocal(rec[:, :, :], src[:, :, :, HD]))
                        if st:
                            link(dve.tensor_scalar(rec[:, :, :], rec[:, :, :], mix_p[0:TT, st - 1:st], None, ALU.mult))
                        if gg == 0:
                            if st == 2:
                                filled(dve, "cT0")
                            if st == 0 and B_ON:
                                filled(dve, "n5T")
                        dst = cx[:, :, :].rearrange("p t (h d) -> p t h d", d=HD)[:, :, 8 * gg:8 * gg + 8, :]
                        read_out(dve.tensor_tensor(dst, src[:, :, :, 0:HD],
                                                   rec[:, :, :].unsqueeze(3).broadcast_to([TT, 2, 8, HD]),
                                                   ALU.mult), name)

                    def mean(i):
                        if i:
                            wait_read(dve, "n5T")
                        dve.tensor_reduce(msum[:, :], nbT[:, :, :], AX.X, ALU.add).then_inc(msum_ready, 1)

                    def logits(i):
                        n, bias = ((2, mix_rb), (EX, ex_rb))[i]
                        name = f"lg{i}"
                        ps = filled(dve, name)
                        read_out(dve.scalar_tensor_tensor(logit[:, 0:n], ps[:, 0:n], 1.0 / TP, bias[:, 0:n],
                                                          ALU.mult, ALU.add), name)
                        wait_read(dve, name)
                        dve.tensor_reduce(neg_max[:, :], logit[:, 0:n], AX.X, ALU.max, negate=True)\
                           .then_inc(logit_ready, 1)

                    def probabilities(i, n, p):
                        dve.wait_ge(softexp_ready, i + 1)
                        link(dve.reciprocal(erec[:, :], esum[:, :]))
                        link(dve.tensor_scalar(p[:, 0:n], expo[:, 0:n], erec[:, 0:1], None, ALU.mult))

                    def mix_weights():
                        probabilities(0, 2, mix_p)

                    def bias_rows():
                        for m in range(2):
                            link(dve.scalar_tensor_tensor(xm[:, :, :], both(bo[:, m, :]), mix_p[0:TT, m:m + 1],
                                                          xm[:, :, :], ALU.mult, ALU.add))

                    def wo_(m):
                        name = f"wo{m}"
                        ps = filled(dve, name)
                        if m:
                            wait_read(dve, "wo0")
                        read_out(dve.tensor_tensor(xm[:, :, :], xm[:, :, :],
                                                   ps[0:TT, :].rearrange("p (t d) -> p t d", t=2), ALU.add), name)

                    def experts_chosen():
                        probabilities(1, EX, ex_p)
                        link(dve.max(ex_v[:, :], ex_p[:, :]))
                        link(dve.max_index(ex_i[:, :], ex_v[:, :], ex_p[:, :]))
                        dve.tensor_copy(ex_o[:, :], ex_i[0:1, :]).then_inc(expert_ready, 1)
                        link(dve.tensor_tensor(pair_sum[:, :], ex_v[:, 0:1], ex_v[:, 1:2], ALU.add))
                        link(dve.reciprocal(pair_rec[:, :], pair_sum[:, :]))
                        link(dve.tensor_scalar(ex_w[:, :], ex_v[:, 0:2], pair_rec[:, 0:1], None, ALU.mult))

                    def hidden_columns(tt, k):
                        name = f"hT{tt}{k}"
                        ps = filled(dve, name)
                        if tt:
                            filled(dve, "y0")
                        read_out(dve.tensor_scalar(hidT[:, k, :, :], ps[:, 0:FK * TT].rearrange("p (c t) -> p c t", c=FK),
                                                   ex_w[:, k:k + 1], None, ALU.mult), name)

                    def expert_sum(tt):
                        ps = filled(dve, f"y{tt}")
                        read_out(dve.tensor_tensor(y[:, tt, :], hb[:, tt, :], ps[0:TT, 0:D], ALU.add), f"y{tt}")

                    walk({"norm": norm, "rows": rows, "batch_norm": batch_norm, "gram_out": gram_,
                          "mean_square_out": mean_square, "diagonals": diagonals, "spread_out": spread,
                          "token_values_out": token_values, "route_out": route_, "gates": gates, "ffn_out": ffn,
                          "stack_out": stack, "v_out": v, "qk_out": qk_, "score_out": score, "max_split": max_split,
                          "weigh_out": weigh, "context_out": context, "mean": mean, "logits_out": logits,
                          "mix_weights": mix_weights, "bias_rows": bias_rows, "wo_out": wo_,
                          "experts_chosen": experts_chosen, "hidden_columns_out": hidden_columns,
                          "expert_sum_out": expert_sum})

                @block.gpsimd
                def _(pool):
                    chain = [0]

                    def link(ins):
                        chain[0] += 1
                        ins.then_inc(pool_chain, 1)
                        pool.wait_ge(pool_chain, chain[0])

                    def norm(i):
                        _, _, eps, count = NORM[i]
                        _, mv, var, var_ready, rstd, rstd_ready, _ = BACK_NORM if i == 6 else FRONT_NORM
                        pool.wait_ge(var_ready, count)
                        link(pool.tensor_scalar(var[:, :], mv[:, :, 1], eps, None, ALU.add))
                        pool.tensor_tensor(rstd[:, :], var[:, :], neg_half[0:TT, :], ALU.pow).then_inc(rstd_ready, 1)

                    def mean_square():
                        wait_read(pool, "ms")
                        pool.tensor_tensor(inv_root[:, :], mean_sq[:, :], neg_half[0:TT, :], ALU.pow)\
                            .then_inc(inv_root_ready, 1)

                    def split(st, tt):
                        pool.wait_ge(hi_ready, 2 * (2 * STACK_POS[st] + tt + 1))
                        pool.tensor_tensor(q_stack[:, :, 2, :], qk[:, tt, 0, :, :], q_stack[:, :, 0, :].bitcast(F32),
                                           ALU.subtract).then_inc(lo_ready, 1)
                        pool.tensor_tensor(k_stack[:, :, 1, :], qk[:, tt, 1, :, :], k_stack[:, :, 0, :].bitcast(F32),
                                           ALU.subtract).then_inc(lo_ready, 1)

                    walk({"norm": norm, "mean_square_out": mean_square, "split": split})

            nc.all_engine_barrier(sems_to_clear=per_iteration)

        iteration(0, None, None)
        iteration(1, 0, None)
        with nc.Fori(0, B - 2) as clip:
            iteration(clip + 2, clip + 1, clip)
        iteration(None, B - 1, B - 2)
        with nc.Block() as block:
            @block.sync
            def _(sp):
                sp.dma_start(out[B - 1, :, :].rearrange("(t p) d -> p t d", p=TT), y).then_inc(y_stored, 16)
                sp.wait_ge(y_stored, 16)


def kernel(**inputs):
    import numpy as np
    import concourse.bacc as bacc
    from concourse.bass_utils import run_bass_kernel_spmd

    w = {name: np.asarray(a) for name, a in inputs.items()}

    def columns(a):
        return a.reshape(-1, 128, a.shape[-1]).transpose(1, 0, 2)

    mha = [[w[f"L1_ffn_mha_{n}"][m].reshape(D, H * HD) for n in ("wq", "wk", "wv")] for m in range(2)]
    qkv = [[w[f"L1_attn_{n}"].T for n in ("Wq", "Wk", "Wv")]] + mha
    arrays = {
        "x": w["x"],
        "conv_w": columns(w["L0_tok_W"].T),
        "conv_rows": np.stack([w["L0_tok_b"], w["L0_tok_gamma"], w["L0_tok_beta"], w["L0_tok_running_mean"]]),
        "bn_var": w["L0_tok_running_var"].reshape(DK, 128).T,
        "keys": columns(w["L0_attn_key_param_tokens"].T),
        "key_rows": columns(w["L0_attn_key_param_tokens"]),
        "values": columns(w["L0_attn_value_param_tokens"]),
        "route": columns(np.concatenate([w["L0_ffn_w_route"], w["L0_ffn_compress"]]).T),
        "routed": w["L0_ffn_routed"].transpose(0, 2, 1).reshape(E * R, D),
        "qkv_w": np.stack([columns(np.concatenate(s, axis=1)) for s in qkv], axis=1),
        "qk_bias": np.stack([np.concatenate([w[f"L1_ffn_mha_{n}"][m].reshape(-1) for n in ("bq", "bk")])
                              for m in range(2)]),
        "bv": np.stack([w["L1_ffn_mha_bv"][m].reshape(DK, 128).T for m in range(2)], axis=1),
        "wo": np.stack([columns(w["L1_ffn_mha_wo"][m].reshape(D, D)) for m in range(2)], axis=1),
        "bo": w["L1_ffn_mha_bo"],
        "ln_cols": np.stack([w[f"L1_ffn_{n}"].reshape(DK, 128).T for n in ("ln1_g", "ln1_b", "ln2_g", "ln2_b")], axis=1),
        "mix_rw": columns(w["L1_ffn_mha_rw"]),
        "mix_rb": w["L1_ffn_mha_rb"].reshape(1, -1),
        "ex_rw": columns(w["L1_ffn_ffn_rw"]),
        "ex_rb": w["L1_ffn_ffn_rb"].reshape(1, -1),
        "fw1": w["L1_ffn_fw1"].reshape(EX, DK, 128, F).transpose(2, 0, 1, 3).reshape(128, EX, DK * F),
        "fw2": w["L1_ffn_fw2"].reshape(EX, FK, 128, D).transpose(2, 0, 1, 3).reshape(128, EX, FK * D),
    }
    arrays = {name: np.ascontiguousarray(a) for name, a in arrays.items()}
    nc = bacc.Bacc("TRN2", target_bir_lowering=False, num_devices=1)
    inp = {name: nc.dram_tensor(f"in_{name}", shape, F32, kind="ExternalInput").ap() for name, shape in INPUTS.items()}
    out = nc.dram_tensor("out", [B, TP, D], F32, kind="ExternalOutput").ap()
    audio_tower(nc, inp, out)
    r = run_bass_kernel_spmd(nc, [{f"in_{name}": a for name, a in arrays.items()}], core_ids=[0])
    return r.results[0]["out"]
```
